# Optimizing a Trainium2 kernel written in Bass

```python
import numpy as np
import jax
import jax.numpy as jnp

def _softmax(x, axis=-1):
    return jax.nn.softmax(x, axis=axis)

def _gelu(x):
    return jax.nn.gelu(x, approximate=True)

def _silu(x):
    return jax.nn.silu(x)

def _sigmoid(x):
    return jax.nn.sigmoid(x)

def _layernorm(x, axis=-1, eps=1e-05):
    m = jnp.mean(x, axis=axis, keepdims=True)
    v = jnp.var(x, axis=axis, keepdims=True)
    return (x - m) / jnp.sqrt(v + eps)

def _scatter_add(tgt, idx, src, axis=0):
    return tgt.at[idx].add(src)

def _segment_sum(src, seg, n):
    return jax.ops.segment_sum(src, seg, n)
kernel_name = 'mk_vit_tower_d1_tok_img1024_r4_5d6909'

def setup_inputs(seed: int=0):
    np.random.seed(seed)
    _w = jnp.asarray

    def _rec_inputs():
        import jax
        import jax.numpy as jnp
        _rk = jax.random.key(seed)
        x = -0.00016672 + 0.999947 * jax.random.normal(jax.random.fold_in(_rk, 1), (16, 3, 96, 96), jnp.float32)
        return x
    x = _rec_inputs()

    def _L0_tok_setup():
        import jax, jax.numpy as jnp
        import numpy as np
        IMG = 96
        PATCH = 16
        CIN = 3
        EMBED = 256
        NP_ = (IMG // PATCH) ** 2
        key = jax.random.key(seed)
        k1, k2, k3, k4, k5 = jax.random.split(key, 5)
        x = jax.random.normal(k1, (64, CIN, IMG, IMG), dtype=jnp.float32)
        d_in = PATCH * PATCH * CIN
        W = jax.random.normal(k2, (d_in, EMBED), dtype=jnp.float32) / np.sqrt(d_in)
        b = jax.random.normal(k3, (EMBED,), dtype=jnp.float32) * 0.01
        class_token = jax.random.normal(k4, (1, 1, EMBED), dtype=jnp.float32)
        pos_emb = jax.random.normal(k5, (1, NP_ + 1, EMBED), dtype=jnp.float32)
        return {'x': x, 'W': W, 'b': b, 'class_token': class_token, 'pos_emb': pos_emb}
    _L0_tok_all = _L0_tok_setup()
    _L0_tok_in = {k: v for k, v in _L0_tok_all.items() if k in ('W', 'b', 'class_token', 'pos_emb')}
    del _L0_tok_all

    def _L0_attn_setup():
        import jax, jax.numpy as jnp
        import numpy as np
        D_MODEL = 256
        N_HEADS = 16
        D_K = D_MODEL // N_HEADS
        WINDOW = 128
        ROPE_BASE = 10000.0

        def _apply_rope(x):
            S, D = (x.shape[2], x.shape[3])
            half = D // 2
            inv_freq = 1.0 / ROPE_BASE ** (jnp.arange(half, dtype=jnp.float32) / half)
            ang = jnp.arange(S, dtype=jnp.float32)[:, None] * inv_freq[None, :]
            cos = jnp.cos(ang).astype(x.dtype)
            sin = jnp.sin(ang).astype(x.dtype)
            x_even = x[..., ::2]
            x_odd = x[..., 1::2]
            out_even = x_even * cos - x_odd * sin
            out_odd = x_odd * cos + x_even * sin
            return jnp.stack([out_even, out_odd], axis=-1).reshape(x.shape)
        key = jax.random.key(seed)
        k1, k2, k3 = jax.random.split(key, 3)
        B, S = (2, 512)
        x = jax.random.normal(k1, (B, S, D_MODEL), dtype=jnp.float32)
        w_qkv = jax.random.normal(k2, (D_MODEL, 3 * D_MODEL), dtype=jnp.float32) * D_MODEL ** (-0.5)
        w_o = jax.random.normal(k3, (D_MODEL, D_MODEL), dtype=jnp.float32) * D_MODEL ** (-0.5)
        return {'x': x, 'w_qkv': w_qkv, 'w_o': w_o}
    _L0_attn_all = _L0_attn_setup()
    _L0_attn_in = {k: v for k, v in _L0_attn_all.items() if k in ('w_qkv', 'w_o')}
    del _L0_attn_all

    def _L0_ffn_setup():
        import jax, jax.numpy as jnp
        import numpy as np
        NUM_KEYS = 128
        TOP_K = 8
        NUM_HEADS = 4
        key = jax.random.key(seed)
        ks = jax.random.split(key, 8)
        b, t, d = (1, 512, 256)
        inter = 512
        E, h, ret = (4096, NUM_HEADS, 64)
        s = 0.02
        return {'hidden_states': jax.random.normal(ks[0], (b, t, d), jnp.float32), 'w_queries': jax.random.normal(ks[1], (h * ret, d), jnp.float32) * s, 'keys': jax.random.normal(ks[2], (h, NUM_KEYS, 2, ret // 2), jnp.float32) * s, 'down_embed': jax.random.normal(ks[3], (E, d), jnp.float32) * s, 'up_embed': jax.random.normal(ks[4], (E, d), jnp.float32) * s, 'w_gate': jax.random.normal(ks[5], (inter, d), jnp.float32) * s, 'w_up': jax.random.normal(ks[6], (inter, d), jnp.float32) * s, 'w_down': jax.random.normal(ks[7], (d, inter), jnp.float32) * s}
    _L0_ffn_all = _L0_ffn_setup()
    _L0_ffn_in = {k: v for k, v in _L0_ffn_all.items() if k in ('w_queries', 'keys', 'down_embed', 'up_embed', 'w_gate', 'w_up', 'w_down')}
    del _L0_ffn_all
    return {'x': x, 'L0_tok_W': _L0_tok_in['W'], 'L0_tok_b': _L0_tok_in['b'], 'L0_tok_class_token': _L0_tok_in['class_token'], 'L0_tok_pos_emb': _L0_tok_in['pos_emb'], 'L0_attn_w_qkv': _L0_attn_in['w_qkv'], 'L0_attn_w_o': _L0_attn_in['w_o'], 'L0_ffn_w_queries': _L0_ffn_in['w_queries'], 'L0_ffn_keys': _L0_ffn_in['keys'], 'L0_ffn_down_embed': _L0_ffn_in['down_embed'], 'L0_ffn_up_embed': _L0_ffn_in['up_embed'], 'L0_ffn_w_gate': _L0_ffn_in['w_gate'], 'L0_ffn_w_up': _L0_ffn_in['w_up'], 'L0_ffn_w_down': _L0_ffn_in['w_down']}

def reference(x, L0_tok_W, L0_tok_b, L0_tok_class_token, L0_tok_pos_emb, L0_attn_w_qkv, L0_attn_w_o, L0_ffn_w_queries, L0_ffn_keys, L0_ffn_down_embed, L0_ffn_up_embed, L0_ffn_w_gate, L0_ffn_w_up, L0_ffn_w_down):
    import jax
    import jax.numpy as jnp

    def _L0_tok_ref(x, W, b, class_token, pos_emb):
        import jax, jax.numpy as jnp
        import numpy as np
        IMG = 96
        PATCH = 16
        CIN = 3
        EMBED = 256
        NP_ = (IMG // PATCH) ** 2
        B = x.shape[0]
        Hp = IMG // PATCH
        patches = x.reshape(B, CIN, Hp, PATCH, Hp, PATCH)
        patches = patches.transpose(0, 2, 4, 1, 3, 5).reshape(B, Hp * Hp, CIN * PATCH * PATCH)
        patch_emb = jnp.einsum('bnd,de->bne', patches, W) + b
        cls = jnp.broadcast_to(class_token, (B, 1, EMBED))
        emb = jnp.concatenate([cls, patch_emb], axis=1) + pos_emb
        return emb

    def _L0_attn_ref(x, w_qkv, w_o):
        import jax, jax.numpy as jnp
        import numpy as np
        D_MODEL = 256
        N_HEADS = 16
        D_K = D_MODEL // N_HEADS
        WINDOW = 128
        ROPE_BASE = 10000.0

        def _apply_rope(x):
            S, D = (x.shape[2], x.shape[3])
            half = D // 2
            inv_freq = 1.0 / ROPE_BASE ** (jnp.arange(half, dtype=jnp.float32) / half)
            ang = jnp.arange(S, dtype=jnp.float32)[:, None] * inv_freq[None, :]
            cos = jnp.cos(ang).astype(x.dtype)
            sin = jnp.sin(ang).astype(x.dtype)
            x_even = x[..., ::2]
            x_odd = x[..., 1::2]
            out_even = x_even * cos - x_odd * sin
            out_odd = x_odd * cos + x_even * sin
            return jnp.stack([out_even, out_odd], axis=-1).reshape(x.shape)
        B, S, _ = x.shape
        qkv = (x @ w_qkv).reshape(B, S, 3, N_HEADS, D_K)
        qkv = jnp.transpose(qkv, (2, 0, 3, 1, 4))
        q, k, v = (qkv[0], qkv[1], qkv[2])
        q = _apply_rope(q)
        k = _apply_rope(k)
        i = jnp.arange(S)[:, None]
        j = jnp.arange(S)[None, :]
        allowed = (j <= i) & (j >= i - WINDOW)
        bias = jnp.where(allowed, 0.0, -jnp.inf).astype(x.dtype)
        scores = jnp.einsum('bhqd,bhkd->bhqk', q, k) * D_K ** (-0.5) + bias
        attn = jax.nn.softmax(scores, axis=-1)
        out = jnp.einsum('bhqk,bhkd->bhqd', attn, v)
        out = jnp.transpose(out, (0, 2, 1, 3)).reshape(B, S, D_MODEL)
        return out @ w_o

    def _L0_ffn_ref(hidden_states, w_queries, keys, down_embed, up_embed, w_gate, w_up, w_down):
        import jax, jax.numpy as jnp
        import numpy as np
        NUM_KEYS = 128
        TOP_K = 8
        NUM_HEADS = 4
        b, t, d = hidden_states.shape
        h, nk, _, n = keys.shape
        k = TOP_K
        q = (hidden_states @ w_queries.T).reshape(b, t, 2, h, n)
        sim = jnp.einsum('btphn,hkpn->pbthk', q, keys)
        sx, ix = jax.lax.top_k(sim[0], k)
        sy, iy = jax.lax.top_k(sim[1], k)
        all_scores = (sx[..., :, None] + sy[..., None, :]).reshape(b, t, h, k * k)
        all_idx = (ix[..., :, None] * nk + iy[..., None, :]).reshape(b, t, h, k * k)
        scores, pos = jax.lax.top_k(all_scores, k)
        indices = jnp.take_along_axis(all_idx, pos, axis=-1)
        de = down_embed[indices]
        ue = up_embed[indices]
        ew = jnp.einsum('btd,bthkd->bthk', hidden_states, de)
        ew = jax.nn.silu(ew) * jax.nn.softmax(scores, axis=-1)
        experts_states = jnp.einsum('bthk,bthkd->btd', ew, ue)
        mlp = jax.nn.silu(hidden_states @ w_gate.T) * (hidden_states @ w_up.T) @ w_down.T
        return mlp + experts_states
    h = _L0_tok_ref(x, L0_tok_W, L0_tok_b, L0_tok_class_token, L0_tok_pos_emb)
    h = h + _L0_attn_ref(_layernorm(h, axis=-1), L0_attn_w_qkv, L0_attn_w_o)
    h = h + _L0_ffn_ref(_layernorm(h, axis=-1), L0_ffn_w_queries, L0_ffn_keys, L0_ffn_down_embed, L0_ffn_up_embed, L0_ffn_w_gate, L0_ffn_w_up, L0_ffn_w_down)
    return h

_drawn_inputs = setup_inputs


def setup_inputs(seed=0):
    import zlib

    import numpy as np

    out = dict(_drawn_inputs(seed))
    spreads = {}
    factors = {'L0_tok_b': 6.404,
     'L0_ffn_w_queries': 8.0,
     'L0_ffn_keys': 8.0,
     'L0_ffn_down_embed': 8.0,
     'L0_ffn_up_embed': 7.739,
     'L0_ffn_w_gate': 3.538,
     'L0_ffn_w_up': 3.481,
     'L0_ffn_w_down': 3.53}
    for name, (base, spread) in spreads.items():
        noise = np.random.default_rng([zlib.crc32(name.encode()), seed]).standard_normal(out[name].shape)
        drawn = base * np.exp(spread * noise) if base else spread * noise
        out[name] = jnp.asarray(drawn.astype(out[name].dtype))
    for name, factor in factors.items():
        out[name] = (out[name] * factor).astype(out[name].dtype)
    return out
```

```python
import concourse.bass as bass
from concourse import mybir
from contextlib import ExitStack

F32 = mybir.dt.float32
F16 = mybir.dt.float16
BF16 = mybir.dt.bfloat16
U32 = mybir.dt.uint32
ALU = mybir.AluOpType
ACT = mybir.ActivationFunctionType
AX = mybir.AxisListType

B, CIN, IMG, PATCH = 16, 3, 96, 16
SIDE = IMG // PATCH
D = 256
S = SIDE * SIDE + 1
T = B * S
KC_TOK = CIN * PATCH * PATCH // 128
DC = D // 128
H, DK = 16, 16
HP = 128 // DK
PER = 111 // S
GROUPS = [(b, min(PER, B - b)) for b in range(0, B, PER)]
ROWS = PER * S
PAIRS = H // 2
FH, NK, FN, TOPK = 4, 128, 32, 8
SLOTS = FH * TOPK
E = 4096
EX = E // NK
INTER = 512
IC = INTER // 128
Q = 4
TQ = T // Q
TQP = 160
TT = 32
TILES = TQP // TT
TP = Q * TQP
BANK = 512
HALF = T // 2
ROUND = BANK // EX
EPS = 1e-5
WSCALE = float(2 ** 14)
NEG = -1e30

C_ID = 0
C_COS = C_ID + 128
C_SIN = C_COS + S
C_CAUSAL = C_SIN + S
C_HEAD = C_CAUSAL + S
C_PAR = C_HEAD + HP
C_IOTA = C_PAR + 2 * DK
C_ALL = C_IOTA + 128


def valid(j):
    return min(TT, TQ - j * TT)


def vit_tower(nc, x, w_tok, b_tok, cls_tok, pos, w_qkv, w_o, w_queries, keys, down_e, up_e,
              w_gate, w_up, w_down, consts, out):
    ctx = ExitStack()
    with ctx:
        def sb(name, shape, dt=F32):
            return ctx.enter_context(nc.sbuf_tensor(name, shape, dt))

        def sem(name):
            return ctx.enter_context(nc.semaphore(name))

        con = sb("con", [128, C_ALL])
        ident = con[:, C_ID:C_ID + 128]
        ident_h = sb("ident_h", [128, 128], BF16)
        causal_h = sb("causal_h", [128, S], BF16)
        iota_h = sb("iota_h", [128, 128], F16)
        wqT = sb("wqT", [128, DC, D])
        keysBD = sb("keysBD", [128, 2, FH, NK])
        gateT = sb("gateT", [128, DC, INTER])
        upT = sb("upT", [128, DC, INTER])
        downT = sb("downT", [128, IC, D])
        ue = sb("ue", [128, EX, D])
        hnT = sb("hnT", [128, DC, TP])
        actT = sb("actT", [128, IC, T])
        de = sb("de", [128, 2, 2, D])
        deT = sb("deT", [128, 2, DC, 128])
        resid = hnT[:, :, :].rearrange("p k t -> p (k t)").rearrange("p (j d) -> p j d", j=TILES)

        big = sb("big", [128, EX * T])
        sil = big[:, :].rearrange("p (e t) -> p e t", e=EX)
        at = 0

        def part(width):
            nonlocal at
            at += width
            assert at <= EX * T
            return big[:, at - width:at]

        tok_words = CIN * PATCH * IMG + KC_TOK * (T + D)
        early = part(tok_words)
        x_sb = early[:, 0:CIN * PATCH * IMG].rearrange("p (c r w) -> p c r w", c=CIN, r=PATCH)
        patchT = early[:, CIN * PATCH * IMG:tok_words - KC_TOK * D].rearrange("p (k t) -> p k t", k=KC_TOK)
        wtok = early[:, tok_words - KC_TOK * D:tok_words].rearrange("p (k n) -> p k n", k=KC_TOK)
        kexp = early[:, 0:2 * B * HP * S].rearrange("p (a b h s) -> p a b h s", a=2, b=B, h=HP)

        RING = 3
        slot_words = RING * TT * (128 + 2 * 32) // 2
        slots = sb("slots", [128, slot_words])
        slots_h = slots[:, :].bitcast(F16)
        R = slots_h[:, 0:RING * TT * 128].rearrange("p (t y) -> p t y", y=128)
        A = slots_h[:, RING * TT * 128:RING * TT * 192].rearrange("p (a t x) -> p a t x", a=2, x=32)
        at2 = 0

        def part2(width):
            nonlocal at2
            at2 += width
            assert at2 <= slot_words
            return slots[:, at2 - width:at2]

        qpad = part2(2 * B * ROWS).rearrange("p (a b r) -> p a b r", a=2, b=B)
        vblk = part2(B * D).rearrange("p (b c) -> p b c", b=B)
        hn_nat = part2(DC * T).rearrange("p (k t) -> p k t", k=DC)
        x_re = slots[:, 2 * B * ROWS:2 * B * ROWS + CIN * PATCH * IMG].rearrange("p (c w n) -> p c w n", c=CIN, w=SIDE)
        xnT = actT[:, :, :].rearrange("p c t -> p (c t)").rearrange("p (k b two s) -> p k b two s", k=DC, b=B, two=2)
        wqkv = part(DC * 3 * D).rearrange("p (k n) -> p k n", k=DC)
        wsw = part(DC * 2 * D).rearrange("p (k n) -> p k n", k=DC)
        wo = part(DC * D).rearrange("p (k n) -> p k n", k=DC)
        posful = part(D)
        addend = part(D)
        h = part(len(GROUPS) * D).rearrange("p (g n) -> p g n", n=D)
        keys_nat = part(FH * 2 * FN).rearrange("p (a h n) -> p a h n", h=FH, a=2)
        pr = part(2 * H * S).rearrange("p (g h s) -> p g h s", g=2, h=H)
        pT = part(2 * PAIRS * ROWS).rearrange("p (g c r) -> p g c r", g=2, c=PAIRS)
        oT = part(2 * 2 * ROWS).rearrange("p (g a r) -> p g a r", g=2, a=2)
        xn = sb("xn", [128, 2, D])
        stats = sb("stats", [128, 6])
        mv = sb("mv", [128, 2])
        rs = sb("rs", [128, 4])
        wq_nat = ue[:, 0:2, :]
        gate_nat = ue[:, 2:6, :]
        up_nat = ue[:, 6:10, :]
        down_nat = ue[:, 10:14, :].rearrange("p a b -> p (a b)").rearrange("p (a b) -> p a b", a=2)
        red = sb("red", [128, 3, H])
        qT = sb("qT", [128, 2, TP])
        top = sb("top", [128, 2, FH, TOPK])
        topi = sb("topi", [128, 2, FH, TOPK], U32)
        topf = sb("topf", [128, 2, FH, TOPK])
        cand = sb("cand", [128, FH, TOPK, TOPK])
        best = sb("best", [128, FH, TOPK])
        besti = sb("besti", [128, FH, TOPK], U32)
        sel = sb("sel", [128, 2, FH, TOPK], U32)
        self_ = sb("self_", [128, 2, FH, TOPK])
        pick = sb("pick", [128, 2, FH, TOPK])
        oneh = sb("oneh", [128, FH, TOPK, TOPK])
        over = sb("over", [128, FH, TOPK])
        ex = sb("ex", [128, FH, TOPK])
        den = sb("den", [128, FH])
        pack = sb("pack", [128, 4, SLOTS], F16)
        packT = sb("packT", [128, TILES, 4, TT], F16)
        eqx = sb("eqx", [128, TT, 32], F16)
        fin = xn
        sg = sb("sg", [128, T])
        rot = qT[:, :, 0:T]
        kT = sg[:, :]

        ps = ctx.enter_context(nc.psum_tensor("ps", [128, 8, 512], F32))

        def flat(bank, width):
            return ps[:, bank:bank + 2, :].rearrange("p a c -> p (a c)")[:, 0:width]

        h_dram = nc.dram_tensor("h_scratch", (T, D), F32, kind="Internal").ap()

        ld_con, ld_x, ld_wtok, ld_pos = sem("ld_con"), sem("ld_x"), sem("ld_wtok"), sem("ld_pos")
        ld_qkv, ld_wo, ld_nat, ld_ue = sem("ld_qkv"), sem("ld_wo"), sem("ld_nat"), sem("ld_ue")
        ld_de = [sem("ld_de0"), sem("ld_de1")]
        ld_res, st_h = sem("ld_res"), sem("st_h")
        st_out = [sem("st_out0"), sem("st_out1")]
        dve_chain, act_chain, pool_chain = sem("dve_chain"), sem("act_chain"), sem("pool_chain")
        s_const, s_zero = sem("s_const"), sem("s_zero")
        pe_nat, act_nat, re_dve, re_act = sem("pe_nat"), sem("act_nat"), sem("re_dve"), sem("re_act")
        pe_patch, patch_dve, patch_act = sem("pe_patch"), sem("patch_dve"), sem("patch_act")
        pe_emb, xn_ready, pe_xn, xnT_ready = sem("pe_emb"), sem("xn_ready"), sem("pe_xn"), sem("xnT_ready")
        sw_ready, pe_qk, rope_done, kT_ready, kexp_dve, kexp_act = (
            sem("sw_ready"), sem("pe_qk"), sem("rope_done"), sem("kT_ready"), sem("kexp_dve"), sem("kexp_act"))
        pe_v, v_ready = sem("pe_v"), sem("v_ready")
        pe_sc, sc_sub, exp_done, prob_ready = sem("pe_sc"), sem("sc_sub"), sem("exp_done"), sem("prob_ready")
        pe_pT, pT_ready, pe_o, oT_ready, pe_wo = (
            sem("pe_pT"), sem("pT_ready"), sem("pe_o"), sem("oT_ready"), sem("pe_wo"))
        hn_ready, pe_hn, hn_nat_ready, hnT_ready, h_ready = (
            sem("hn_ready"), sem("pe_hn"), sem("hn_nat_ready"), sem("hnT_ready"), sem("h_ready"))
        pe_q, qT_ready, pe_sim, sim_read = sem("pe_q"), sem("qT_ready"), sem("pe_sim"), sem("sim_read")
        pe_gu, gate_act, gu_done = sem("pe_gu"), sem("gate_act"), sem("gu_done")
        pe_deT, deT_ready, pe_s, sil_ready = sem("pe_deT"), sem("deT_ready"), sem("pe_s"), sem("sil_ready")
        lg_ready, lg_exp, slots_ready = sem("lg_ready"), sem("lg_exp"), sem("slots_ready")
        pe_p, g_ready, pe_out, fin_ready = sem("pe_p"), sem("g_ready"), sem("pe_out"), sem("fin_ready")

        NG = len(GROUPS)
        NPOS = 2 * PER
        block = ctx.enter_context(nc.Block())

        @block.sync
        def _(sp):
            for r in range(0, SIDE, 2):
                sp.dma_start(x_sb[r * B:(r + 1) * B], x[:, :, r * PATCH:(r + 1) * PATCH, :]).then_inc(ld_x, 16)
            sp.dma_start(wtok[:, :, :], w_tok.rearrange("(k p) n -> p k n", p=128)).then_inc(ld_wtok, 16)
            for i in range(PER):
                sp.dma_start(addend[i * S:i * S + 1, :], cls_tok[0, :, :]).then_inc(ld_pos, 16)
                sp.dma_start(addend[i * S + 1:(i + 1) * S, :],
                             b_tok.rearrange("(a n) -> a n", a=1).broadcast_to([S - 1, D])).then_inc(ld_pos, 16)
                sp.dma_start(posful[i * S:(i + 1) * S, :], pos[0, :, :]).then_inc(ld_pos, 16)
            sp.dma_start(wqkv[:, :, :], w_qkv.rearrange("(k p) n -> p k n", p=128)).then_inc(ld_qkv, 16)
            sp.dma_start(wo[:, :, :], w_o.rearrange("(k p) n -> p k n", p=128)).then_inc(ld_wo, 16)
            sp.wait_ge(pe_nat, 10)
            up_v = up_e.rearrange("(e p) n -> p e n", p=128)
            for c in range(4):
                w = EX // 4
                sp.dma_start(ue[:, c * w:(c + 1) * w, :], up_v[:, c * w:(c + 1) * w, :]).then_inc(ld_ue, 16)
            for gi, (b0, n) in enumerate(GROUPS):
                sp.wait_ge(h_ready, gi + 1)
                sp.dma_start(h_dram[b0 * S:(b0 + n) * S, :], h[0:n * S, gi, :]).then_inc(st_h, 16)
            sp.wait_ge(st_h, 16 * NG)
            sp.wait_ge(pe_s, EX)
            for j in range(TILES):
                v = valid(j)
                for g in range(Q):
                    t0 = g * TQ + j * TT
                    sp.dma_start(resid[g * v:(g + 1) * v, j, :], h_dram[t0:t0 + v, :]).then_inc(ld_res, 16)
            for j in range(TILES):
                v = valid(j)
                sp.wait_ge(fin_ready, j + 1)
                for g in range(Q):
                    t0 = g * TQ + j * TT
                    sp.dma_start(out[t0:t0 + v, :], fin[g * v:(g + 1) * v, j % 2, :]).then_inc(st_out[j % 2], 16)
            for i in range(2):
                sp.wait_ge(st_out[i], 16 * Q * len(range(i, TILES, 2)))

        @block.gpsimd
        def _(pool):
            nc.gpsimd.memset(patchT.rearrange("p k (b s) -> p k b s", s=S)[:, :, :, 0:1], 0.0).then_inc(s_zero, 1)
            nc.gpsimd.memset(qpad, 0.0).then_inc(s_zero, 1)
            nc.gpsimd.memset(keysBD[:, :, :, :], 0.0).then_inc(s_zero, 1)
            nc.gpsimd.memset(hnT[:, :, 4 * 128:TP], 0.0).then_inc(s_zero, 1)
            for e2 in range(EX // 2):
                if e2 >= 2:
                    pool.wait_ge(pe_deT, 2 * (e2 - 1))
                pool.dma_start(de[:, e2 % 2, :, :],
                               down_e[e2 * 256:(e2 + 1) * 256, :].rearrange("(a p) n -> p a n", p=128)
                               ).then_inc(ld_de[e2 % 2], 16)

        @block.scalar
        def _(act):
            for r in range(1, SIDE, 2):
                act.dma_start(x_sb[r * B:(r + 1) * B], x[:, :, r * PATCH:(r + 1) * PATCH, :]).then_inc(ld_x, 16)
            act.dma_start(con[:, :], consts[:, :]).then_inc(ld_con, 16)
            act.dma_start(wq_nat, w_queries.rearrange("(a p) n -> p a n", p=128)).then_inc(ld_nat, 16)
            act.dma_start(gate_nat, w_gate.rearrange("(a p) n -> p a n", p=128)).then_inc(ld_nat, 16)
            act.dma_start(up_nat, w_up.rearrange("(a p) n -> p a n", p=128)).then_inc(ld_nat, 16)
            act.dma_start(down_nat, w_down.rearrange("(a p) n -> p a n", p=128)).then_inc(ld_nat, 16)
            for p in range(2):
                act.dma_start(keys_nat[:, p], keys[:, :, p, :].rearrange("h k n -> k h n")).then_inc(ld_nat, 16)
            act.wait_ge(ld_con, 16)
            nc.scalar.copy(ident_h[:, :], ident).then_inc(s_const, 1)
            nc.scalar.copy(causal_h[:, :], con[:, C_CAUSAL:C_CAUSAL + S]).then_inc(s_const, 1)
            nc.scalar.copy(iota_h[:, :], con[:, C_IOTA:C_IOTA + 128]).then_inc(s_const, 1)
            act.wait_ge(ld_x, 16 * SIDE)
            for w in range(SIDE):
                nc.scalar.copy(x_re[0:SIDE * B, CIN - 1, w, :].rearrange("p (r n) -> p r n", r=PATCH),
                               x_sb[0:SIDE * B, CIN - 1, :, w * PATCH:(w + 1) * PATCH]).then_inc(re_act, 1)
            act.wait_ge(s_zero, 1)
            for u in range(1, 2 * KC_TOK, 2):
                act.wait_ge(pe_patch, u + 1)
                kc, half = divmod(u, 2)
                dst = patchT[:, kc, :].rearrange("p (b s) -> p b s", s=S)[:, :, 1:]
                dst = dst.rearrange("p b (r c) -> p c r b", c=SIDE)[:, 3 * half:3 * half + 3]
                nc.scalar.copy(dst, ps[:, u % 4, 0:3 * SIDE * B].rearrange("p (c r b) -> p c r b", c=3, b=B)
                               ).then_inc(patch_act, 1)
            act.wait_ge(ld_qkv, 16)
            for k in range(DC):
                pair = wqkv[:, k, 0:2 * D].rearrange("p (c two) -> p c two", two=2)
                twin = wsw[:, k, :].rearrange("p (c two) -> p c two", two=2)
                nc.scalar.mul(twin[:, :, 0], pair[:, :, 1], -1.0).then_inc(sw_ready, 1)
                nc.scalar.copy(twin[:, :, 1], pair[:, :, 0]).then_inc(sw_ready, 1)
            for gi, (b0, n) in enumerate(GROUPS):
                act.wait_ge(pe_xn, gi + 1)
                r = n * S
                for i in range(2):
                    nc.scalar.copy(xnT[:, :, b0:b0 + n, i, :],
                                   ps[:, 6 + gi % 2, 0:2 * r].rearrange("p (k b s) -> p k b s", k=2, s=S)
                                   ).then_inc(xnT_ready, 1)
            for u in range(8):
                act.wait_ge(pe_nat, u + 1)
                src = ps[:, u % 2, :].rearrange("p (a b) -> p a b", a=4)
                if u == 0:
                    dst = wqT[:, :, :].rearrange("p k (a b) -> p (k a) b", a=2)
                elif u < 3:
                    dst = gateT[:, u - 1, :].rearrange("p (a b) -> p a b", a=4)
                elif u < 5:
                    dst = upT[:, u - 3, :].rearrange("p (a b) -> p a b", a=4)
                elif u < 7:
                    dst = downT[:, 2 * (u - 5):2 * (u - 5) + 2, :].rearrange("p k (a b) -> p (k a) b", a=2)
                else:
                    dst = None
                if dst is not None:
                    nc.scalar.copy(dst, src).then_inc(act_nat, 1)
                else:
                    act.wait_ge(s_zero, 3)
                    for hh in range(FH):
                        nc.scalar.copy(keysBD[32 * hh:32 * hh + 32, :, hh, :],
                                       ps[32 * hh:32 * hh + 32, u % 2, 0:256].rearrange("p (a b) -> p a b", a=2)
                                       ).then_inc(act_nat, 1)
            for a in range(2):
                act.wait_ge(kT_ready, a + 1)
                for hh in range(1, HP, 2):
                    nc.scalar.mul(kexp[:, a, :, hh, :], kT.rearrange("p (b s) -> p b s", s=S),
                                  con[:, C_HEAD + hh:C_HEAD + hh + 1]).then_inc(kexp_act, 1)
            for gi, (b0, n) in enumerate(GROUPS):
                r = n * S
                act.wait_ge(sc_sub, gi + 1)
                nc.scalar.activation(pr[0:r, gi % 2], pr[0:r, gi % 2], ACT.Exp,
                                     scale=DK ** -0.5).then_inc(exp_done, 1)
                act.wait_ge(pe_pT, gi + 1)
                nc.scalar.copy(pT[0:2 * S, gi % 2, :, 0:r].rearrange("p (a c) r -> p a c r", a=2),
                               ps[0:2 * S, 2:4, 0:4 * r].rearrange("p a (c r) -> p a c r", c=4)
                               ).then_inc(pT_ready, 1)
                act.wait_ge(pe_o, gi + 1)
                nc.scalar.copy(oT[:, gi % 2, :, 0:r], ps[:, 4:6, 0:r]).then_inc(oT_ready, 1)
                act.wait_ge(pe_hn, gi + 1)
                nc.scalar.copy(hn_nat[:, :, b0 * S:b0 * S + r],
                               ps[:, 7, 0:2 * r].rearrange("p (k t) -> p k t", k=2)).then_inc(hn_nat_ready, 1)
            act.wait_ge(s_zero, 4)
            act.wait_ge(hn_nat_ready, NG)
            for j in range(TILES):
                v = valid(j)
                nc.scalar.copy(hnT[:, :, j * 128:(j + 1) * 128].rearrange("p k (q t) -> p k q t", q=Q)[:, :, :, 0:v],
                               hn_nat.rearrange("p k (q t) -> p k q t", q=Q)[:, :, :, j * TT:j * TT + v]
                               ).then_inc(hnT_ready, 1)
            for p in range(2):
                act.wait_ge(pe_q, p + 1)
                nc.scalar.copy(qT[:, p, :], flat(2 * p, TP)).then_inc(qT_ready, 1)
            for c in range(IC):
                act.wait_ge(pe_gu, c + 1)
                if c >= 2:
                    act.wait_ge(gu_done, c - 1)
                nc.scalar.activation(sg[:, :], flat(0, T), ACT.Silu).then_inc(gate_act, 1)
            for e in range(EX):
                act.wait_ge(pe_deT, e + 1)
                if e >= 2:
                    act.wait_ge(pe_s, e - 1)
                nc.scalar.copy(deT[:, e % 2, :, :],
                               ps[:, e % 2, 0:D].rearrange("p (k y) -> p k y", k=DC)).then_inc(deT_ready, 1)
                if e == 1:
                    act.wait_ge(st_h, 16 * NG)
                if e >= 1:
                    act.wait_ge(pe_s, e)
                    nc.scalar.activation(sil[:, e - 1, :], flat(2 + 2 * ((e - 1) % 2), T), ACT.Silu).then_inc(sil_ready, 1)
                if e % 6 == 5 and e // 6 < TILES:
                    act.wait_ge(lg_ready, e // 6 + 1)
                    nc.scalar.activation(ex[:, :, :], ex[:, :, :], ACT.Exp).then_inc(lg_exp, 1)
            act.wait_ge(pe_s, EX)
            nc.scalar.activation(sil[:, EX - 1, :], flat(4, T), ACT.Silu).then_inc(sil_ready, 1)

        @block.vector
        def _(dve):
            counts, newest = {}, []

            def chain(ins, then=dve_chain):
                counts[then] = counts.get(then, 0) + 1
                ins.then_inc(then, 1)
                newest[:] = [(then, counts[then])]

            def behind():
                dve.wait_ge(*newest[0])

            def norm(rows, src, dst, then):
                behind()
                chain(nc.vector.bn_stats(stats[0:rows, :], src))
                behind()
                chain(nc.vector.bn_aggr(mv[0:rows, :], stats[0:rows, :]))
                behind()
                v, nhalf, y, a = (rs[0:rows, i:i + 1] for i in range(4))
                bits = rs[:, :].bitcast(mybir.dt.int32)
                chain(nc.vector.tensor_scalar(v, mv[0:rows, 1:2], EPS, None, ALU.add))
                behind()
                chain(nc.vector.tensor_scalar(nhalf, v, -0.5, None, ALU.mult))
                chain(nc.vector.tensor_scalar(bits[0:rows, 3:4], bits[0:rows, 0:1], 1, None,
                                              ALU.logical_shift_right))
                behind()
                chain(nc.vector.tensor_scalar(bits[0:rows, 2:3], bits[0:rows, 3:4], -1.0, float(0x5f3759df),
                                              ALU.mult, ALU.add))
                for _ in range(3):
                    behind()
                    chain(nc.vector.scalar_tensor_tensor(a, y, nhalf, y, ALU.mult, ALU.mult))
                    behind()
                    chain(nc.vector.scalar_tensor_tensor(y, a, 1.5, y, ALU.add, ALU.mult))
                behind()
                chain(nc.vector.tensor_scalar(dst, src, mv[0:rows, 0:1], y,
                                              ALU.subtract, ALU.mult), then)

            dve.wait_ge(ld_x, 16 * SIDE)
            for c in range(CIN - 1):
                for w in range(SIDE):
                    chain(nc.vector.tensor_copy(x_re[0:SIDE * B, c, w, :].rearrange("p (r n) -> p r n", r=PATCH),
                                                x_sb[0:SIDE * B, c, :, w * PATCH:(w + 1) * PATCH]), re_dve)
            dve.wait_ge(ld_pos, 16 * 3 * PER)
            chain(nc.vector.tensor_tensor(posful[0:ROWS, :], posful[0:ROWS, :], addend[0:ROWS, :], ALU.add))
            dve.wait_ge(s_zero, 1)
            for u in range(0, 2 * KC_TOK, 2):
                dve.wait_ge(pe_patch, u + 1)
                kc = u // 2
                dst = patchT[:, kc, :].rearrange("p (b s) -> p b s", s=S)[:, :, 1:]
                dst = dst.rearrange("p b (r c) -> p c r b", c=SIDE)[:, 0:3]
                chain(nc.vector.tensor_copy(dst, ps[:, u % 4, 0:3 * SIDE * B]
                                            .rearrange("p (c r b) -> p c r b", c=3, b=B)), patch_dve)
            for gi, (b0, n) in enumerate(GROUPS):
                r = n * S
                dve.wait_ge(pe_emb, gi + 1)
                behind()
                chain(nc.vector.tensor_tensor(h[0:r, gi, :], ps[0:r, 4 + gi % 2, 0:D], posful[0:r, :], ALU.add))
                if gi >= 2:
                    dve.wait_ge(pe_xn, gi - 1)
                norm(r, h[0:r, gi, :], xn[0:r, gi % 2, :], xn_ready)
            cosb = con[:, C_COS:C_COS + S].unsqueeze(1).unsqueeze(1).broadcast_to([128, 2, B // 2, S])
            sinb = con[:, C_SIN:C_SIN + S].unsqueeze(1).unsqueeze(1).broadcast_to([128, 2, B // 2, S])
            for u in range(4):
                half = u % 2
                dve.wait_ge(pe_qk, u + 1)
                k0 = 4 * (u % 2)
                plain = ps[:, k0:k0 + 2, 0:HALF].rearrange("p a (b s) -> p a b s", s=S)
                twin = ps[:, k0 + 2:k0 + 4, 0:HALF].rearrange("p a (b s) -> p a b s", s=S)
                behind()
                chain(nc.vector.tensor_tensor(rot[:, 0, :].rearrange("p (a b s) -> p a b s", a=2, s=S),
                                              plain, cosb, ALU.mult))
                chain(nc.vector.tensor_tensor(rot[:, 1, :].rearrange("p (a b s) -> p a b s", a=2, s=S),
                                              twin, sinb, ALU.mult), rope_done)
                behind()
                if u < 2:
                    if u == 0:
                        dve.wait_ge(s_zero, 2)
                    nb = B - B % PER
                    v = [rot[:, i, 0:nb * S].rearrange("p (g i s) -> p g i s", i=PER, s=S) for i in (0, 1)]
                    base = qpad[:, half, 0:nb, :].rearrange("p (g i) r -> p g i r", i=PER)
                    for i in range(PER):
                        chain(nc.vector.tensor_tensor(base[:, :, i, i * S:(i + 1) * S], v[0][:, :, i, :],
                                                      v[1][:, :, i, :], ALU.add))
                    chain(nc.vector.tensor_tensor(qpad[:, half, nb:B, 0:S],
                                                  rot[:, 0, nb * S:].rearrange("p (b s) -> p b s", s=S),
                                                  rot[:, 1, nb * S:].rearrange("p (b s) -> p b s", s=S), ALU.add))
                else:
                    if half == 1:
                        dve.wait_ge(kexp_act, HP // 2)
                    chain(nc.vector.tensor_tensor(kT, rot[:, 0, :], rot[:, 1, :], ALU.add), kT_ready)
                    behind()
                    for hh in range(0, HP, 2):
                        chain(nc.vector.tensor_scalar(kexp[:, half, :, hh, :], kT.rearrange("p (b s) -> p b s", s=S),
                                                      con[:, C_HEAD + hh:C_HEAD + hh + 1], None, ALU.mult), kexp_dve)
            par = con[0:2 * S, C_PAR:C_PAR + 2 * DK].unsqueeze(1).broadcast_to([2 * S, 2 * PAIRS, 2 * DK])
            for u in range(B // 2):
                dve.wait_ge(pe_v, u + 1)
                chain(nc.vector.tensor_tensor(
                    vblk[0:2 * S, 2 * u:2 * u + 2, :].rearrange("p b (c d) -> p (b c) d", d=2 * DK),
                    ps[0:2 * S, u % 4, :].rearrange("p (c d) -> p c d", d=2 * DK), par, ALU.mult), v_ready)

            def softmax_front(gi):
                r = GROUPS[gi][1] * S
                dve.wait_ge(pe_sc, gi + 1)
                sc = ps[0:r, 0:2, 0:HALF].rearrange("p a (h s) -> p a h s", s=S)
                behind()
                chain(nc.vector.tensor_reduce(red[0:r, 0, :].rearrange("p (a h) -> p a h", a=2), sc, AX.X, ALU.max))
                behind()
                chain(nc.vector.tensor_tensor(pr[0:r, gi % 2].rearrange("p (a h) s -> p a h s", a=2), sc,
                                              red[0:r, 0, :].rearrange("p (a h) -> p a h", a=2).unsqueeze(3)
                                              .broadcast_to([r, 2, HP, S]), ALU.subtract), sc_sub)

            def softmax_back(gi):
                r = GROUPS[gi][1] * S
                dve.wait_ge(exp_done, gi + 1)
                behind()
                chain(nc.vector.tensor_reduce(red[0:r, 1, :], pr[0:r, gi % 2], AX.X, ALU.add))
                behind()
                chain(nc.vector.reciprocal(red[0:r, 2, :], red[0:r, 1, :]))
                behind()
                chain(nc.vector.tensor_tensor(pr[0:r, gi % 2], pr[0:r, gi % 2],
                                              red[0:r, 2, :].unsqueeze(2).broadcast_to([r, H, S]), ALU.mult),
                      prob_ready)

            for gi, (b0, n) in enumerate(GROUPS):
                r = n * S
                softmax_front(gi)
                softmax_back(gi)
                dve.wait_ge(pe_wo, gi + 1)
                behind()
                chain(nc.vector.tensor_tensor(h[0:r, gi, :], ps[0:r, 6, 0:D], h[0:r, gi, :], ALU.add), h_ready)
                if gi >= 1:
                    dve.wait_ge(pe_hn, gi)
                norm(r, h[0:r, gi, :], xn[0:r, gi % 2, :], hn_ready)

            for c in range(IC):
                dve.wait_ge(gate_act, c + 1)
                chain(nc.vector.scalar_tensor_tensor(actT[:, c, :], sg[:, :], WSCALE, flat(2, T), ALU.mult,
                                                     ALU.mult), gu_done)
            iota8 = con[:, C_IOTA:C_IOTA + TOPK]

            def build_slots(j):
                v = valid(j)
                if j >= RING:
                    dve.wait_ge(pe_p, sum(-(-valid(i) // ROUND) for i in range(j - RING + 1)))
                ts = slice((j % RING) * TT, (j % RING) * TT + v)
                behind()
                chain(nc.vector.tensor_tensor(R[:, ts, :], iota_h[:, :].unsqueeze(1).broadcast_to([128, v, 128]),
                                              packT[:, j, 1, 0:v].unsqueeze(2).broadcast_to([128, v, 128]),
                                              ALU.is_equal))
                chain(nc.vector.tensor_tensor(eqx[:, 0:v, :], iota_h[:, 0:32].unsqueeze(1).broadcast_to([128, v, 32]),
                                              packT[:, j, 0, 0:v].unsqueeze(2).broadcast_to([128, v, 32]),
                                              ALU.is_equal))
                behind()
                for a in range(2):
                    chain(nc.vector.tensor_tensor(A[:, a, ts, :], eqx[:, 0:v, :],
                                                  packT[:, j, 2 + a, 0:v].unsqueeze(2).broadcast_to([128, v, 32]),
                                                  ALU.mult), slots_ready)

            for j in range(TILES):
                for p in range(2):
                    dve.wait_ge(pe_sim, 2 * j + p + 1)
                    simv = ps[:, 6 + p, :].rearrange("p (h k) -> p h k", h=FH)
                    behind()
                    for hh in range(FH):
                        chain(nc.vector.max(top[:, p, hh, :], simv[:, hh, :]))
                    behind()
                    for hh in range(FH):
                        chain(nc.vector.max_index(topi[:, p, hh, :], top[:, p, hh, :], simv[:, hh, :]),
                              sim_read if hh == FH - 1 else dve_chain)
                behind()
                chain(nc.vector.tensor_copy(topf[:, :, :, :], topi[:, :, :, :]))
                chain(nc.vector.tensor_tensor(cand[:, :, :, :],
                                              top[:, 0].unsqueeze(3).broadcast_to([128, FH, TOPK, TOPK]),
                                              top[:, 1].unsqueeze(2).broadcast_to([128, FH, TOPK, TOPK]), ALU.add))
                behind()
                cf = cand[:, :, :, :].rearrange("p h i j -> p h (i j)")
                for hh in range(FH):
                    chain(nc.vector.max(best[:, hh, :], cf[:, hh, :]))
                behind()
                for hh in range(FH):
                    chain(nc.vector.max_index(besti[:, hh, :], best[:, hh, :], cf[:, hh, :]))
                chain(nc.vector.tensor_tensor(ex[:, :, :], best[:, :, :],
                                              best[:, :, 0:1].broadcast_to([128, FH, TOPK]), ALU.subtract), lg_ready)
                behind()
                chain(nc.vector.tensor_scalar(sel[:, 0], besti[:, :, :], 3, None, ALU.logical_shift_right))
                chain(nc.vector.tensor_scalar(sel[:, 1], besti[:, :, :], TOPK - 1, None, ALU.bitwise_and))
                behind()
                chain(nc.vector.tensor_copy(self_[:, :, :, :], sel[:, :, :, :]))
                for p in range(2):
                    behind()
                    chain(nc.vector.tensor_tensor(oneh[:, :, :, :],
                                                  self_[:, p].unsqueeze(3).broadcast_to([128, FH, TOPK, TOPK]),
                                                  iota8.unsqueeze(1).unsqueeze(1).broadcast_to([128, FH, TOPK, TOPK]),
                                                  ALU.is_equal))
                    behind()
                    chain(nc.vector.tensor_tensor(oneh[:, :, :, :], oneh[:, :, :, :],
                                                  topf[:, p].unsqueeze(2).broadcast_to([128, FH, TOPK, TOPK]),
                                                  ALU.mult))
                    behind()
                    chain(nc.vector.tensor_reduce(pick[:, p], oneh[:, :, :, :], AX.X, ALU.add))
                behind()
                chain(nc.vector.tensor_scalar(over[:, :, :], pick[:, 0], float(EX), float(NK - 1), ALU.is_ge, ALU.mult))
                chain(nc.vector.tensor_scalar(pack[:, 0, :].rearrange("p (h k) -> p h k", h=FH), pick[:, 0],
                                              float(EX - 1), None, ALU.min))
                behind()
                chain(nc.vector.tensor_tensor(pack[:, 1, :].rearrange("p (h k) -> p h k", h=FH), pick[:, 1],
                                              over[:, :, :], ALU.max))
                dve.wait_ge(lg_exp, j + 1)
                chain(nc.vector.tensor_reduce(den[:, :], ex[:, :, :], AX.X, ALU.add))
                behind()
                chain(nc.vector.reciprocal(den[:, :], den[:, :]))
                behind()
                chain(nc.vector.scalar_tensor_tensor(ex[:, :, :], ex[:, :, :], WSCALE,
                                                     den[:, :].unsqueeze(2).broadcast_to([128, FH, TOPK]),
                                                     ALU.mult, ALU.mult))
                behind()
                wh = pack[:, 2, :].rearrange("p (h k) -> p h k", h=FH)
                chain(nc.vector.tensor_copy(wh, ex[:, :, :]))
                behind()
                chain(nc.vector.tensor_tensor(pack[:, 3, :].rearrange("p (h k) -> p h k", h=FH), ex[:, :, :], wh,
                                              ALU.subtract))
                behind()
                chain(nc.vector.transpose(packT[:, j], pack[:, :, :]))
                if j < RING:
                    build_slots(j)
            dve.wait_ge(sil_ready, EX)
            n_p = 0

            def finish(j):
                v = valid(j)
                dve.wait_ge(pe_out, j + 1)
                if j == 0:
                    dve.wait_ge(ld_res, 16 * Q * TILES)
                if j >= 2:
                    dve.wait_ge(st_out[j % 2], 16 * Q * (j // 2))
                chain(nc.vector.scalar_tensor_tensor(fin[0:Q * v, j % 2, :], ps[0:Q * v, 4 + j % 2, 0:D],
                                                     1.0 / WSCALE, resid[0:Q * v, j, :], ALU.mult, ALU.add),
                      fin_ready)

            for j in range(TILES):
                for t0 in range(0, valid(j), ROUND):
                    w = min(ROUND, valid(j) - t0)
                    dve.wait_ge(pe_p, n_p + 1)
                    pv = ps[:, 0:4, 0:32 * w].rearrange("p q (t e) -> p q e t", e=EX)
                    dst = sil[:, :, j * 128:j * 128 + Q * valid(j)].rearrange("p e (q t) -> p q e t", q=Q)
                    dst = dst[:, :, :, t0:t0 + w]
                    behind()
                    chain(nc.vector.tensor_tensor(dst, pv, dst, ALU.mult), g_ready)
                    n_p += 1
                if j + RING < TILES:
                    build_slots(j + RING)
                if j >= 1:
                    finish(j - 1)
            finish(TILES - 1)

        @block.tensor
        def _(pe):
            mm, tr = nc.tensor.matmul, nc.tensor.transpose
            pe.wait_ge(ld_con, 16)
            for u in range(2 * KC_TOK):
                kc, half = divmod(u, 2)
                c, px = kc // 2, slice(128 * (kc % 2), 128 * (kc % 2) + 128)
                if kc % 2 == 0 and half == 0:
                    if c < CIN - 1:
                        pe.wait_ge(re_dve, SIDE * (c + 1))
                    else:
                        pe.wait_ge(re_act, SIDE)
                if u >= 4:
                    pe.wait_ge((patch_dve, patch_act)[u % 2], u // 2 - 1)
                for wp in range(3):
                    last = tr(ps[:, u % 4, wp * SIDE * B:(wp + 1) * SIDE * B],
                              x_re[0:SIDE * B, c, 3 * half + wp, px], ident[0:SIDE * B, 0:SIDE * B])
                last.then_inc(pe_patch, 1)
            pe.wait_ge(patch_dve, KC_TOK)
            pe.wait_ge(patch_act, KC_TOK)
            pe.wait_ge(ld_wtok, 16)

            def rows_T(gi, ready, bank, done):
                r = GROUPS[gi][1] * S
                pe.wait_ge(ready, gi + 1)
                for k in range(DC):
                    last = tr(ps[:, bank, k * r:(k + 1) * r], xn[0:r, gi % 2, k * 128:(k + 1) * 128],
                              ident[0:r, 0:r])
                last.then_inc(done, 1)

            for gi, (b0, n) in enumerate(GROUPS):
                r = n * S
                if gi >= 2:
                    pe.wait_ge(xn_ready, gi - 1)
                for k in range(KC_TOK):
                    last = mm(ps[0:r, 4 + gi % 2, 0:D], patchT[:, k, b0 * S:b0 * S + r], wtok[:, k, :],
                              start=(k == 0), stop=(k == KC_TOK - 1))
                last.then_inc(pe_emb, 1)
                if gi >= 1:
                    if gi >= 3:
                        pe.wait_ge(xnT_ready, 2 * (gi - 2))
                    rows_T(gi - 1, xn_ready, 6 + (gi - 1) % 2, pe_xn)
            pe.wait_ge(xnT_ready, 2 * (NG - 2))
            rows_T(NG - 1, xn_ready, 6 + (NG - 1) % 2, pe_xn)
            pe.wait_ge(ld_nat, 16 * 6)
            blocks = []
            blocks.append([wq_nat[:, a, k * 128:(k + 1) * 128] for k in range(2) for a in range(2)])
            for src in (gate_nat, up_nat):
                for k in range(2):
                    blocks.append([src[:, a, k * 128:(k + 1) * 128] for a in range(4)])
            for k2 in range(2):
                blocks.append([down_nat[:, a, k * 128:(k + 1) * 128] for k in (2 * k2, 2 * k2 + 1) for a in range(2)])
            blocks.append([keys_nat[:, p].rearrange("p h n -> p (h n)") for p in range(2)])
            for u, bl in enumerate(blocks):
                if u >= 2:
                    pe.wait_ge(act_nat, u - 1)
                for i, src in enumerate(bl):
                    last = tr(ps[:, u % 2, i * 128:(i + 1) * 128], src, ident)
                last.then_inc(pe_nat, 3 if u == len(blocks) - 1 else 1)
            pe.wait_ge(xnT_ready, 2 * NG)
            pe.wait_ge(sw_ready, 2 * DC)
            pe.wait_ge(act_nat, 7 + FH)
            for u in range(4):
                if u >= 2:
                    pe.wait_ge(rope_done, u - 1)
                for i, w in enumerate((wqkv, wsw)):
                    for a in range(2):
                        for k in range(DC):
                            last = mm(ps[:, 4 * (u % 2) + 2 * i + a, 0:HALF], w[:, k, u * 128:(u + 1) * 128],
                                      xnT[:, k, a * (B // 2):(a + 1) * (B // 2), 0, :], start=(k == 0), stop=(k == DC - 1))
                last.then_inc(pe_qk, 1)
            for u in range(B // 2):
                if u == 0:
                    pe.wait_ge(rope_done, 4)
                if u >= 4:
                    pe.wait_ge(v_ready, u - 3)
                for i in range(2):
                    b = 2 * u + i
                    for k in range(DC):
                        twice = xnT[:, k, b, :, :].rearrange("p two s -> p (two s)")
                        last = mm(ps[0:2 * S, u % 4, i * D:(i + 1) * D], twice, wqkv[:, k, 2 * D:3 * D],
                                  start=(k == 0), stop=(k == DC - 1))
                last.then_inc(pe_v, 1)
            pe.wait_ge(v_ready, B // 2)
            pe.wait_ge(kexp_dve, HP)
            pe.wait_ge(kexp_act, HP)
            pe.wait_ge(s_const, 3)
            pe.wait_ge(ld_wo, 16)

            def scores(gi):
                b0, n = GROUPS[gi]
                r = n * S
                if gi >= 1:
                    pe.wait_ge(sc_sub, gi)
                for a in range(2):
                    mm(ps[0:r, a, 0:HALF], ident_h[0:r, 0:r],
                       causal_h[0:r, :].unsqueeze(1).broadcast_to([r, HP, S]), start=True, stop=False)
                    for i in range(n):
                        last = mm(ps[0:r, a, 0:HALF], qpad[:, a, b0 + i, 0:r],
                                  kexp[:, a, b0 + i].rearrange("p h s -> p (h s)"), start=False, stop=(i == n - 1))
                last.then_inc(pe_sc, 1)

            def attend(gi):
                b0, n = GROUPS[gi]
                r = n * S
                pe.wait_ge(prob_ready, gi + 1)
                if gi >= 1:
                    pe.wait_ge(pT_ready, gi)
                for c in range(PAIRS):
                    last = tr(ps[0:2 * S, 2 + c // 4, (c % 4) * r:(c % 4 + 1) * r],
                              pr[0:r, gi % 2, 2 * c:2 * c + 2, :].rearrange("p h s -> p (h s)"), ident[0:r, 0:r])
                last.then_inc(pe_pT, 1)
                pe.wait_ge(pT_ready, gi + 1)
                if gi >= 1:
                    pe.wait_ge(oT_ready, gi)
                for i in range(n):
                    for c in range(PAIRS):
                        p0 = 32 * (c % 4)
                        last = mm(ps[p0:p0 + 32, 4 + c // 4, i * S:(i + 1) * S],
                                  vblk[0:2 * S, b0 + i, 32 * c:32 * c + 32],
                                  pT[0:2 * S, gi % 2, c, i * S:(i + 1) * S], start=True, stop=True,
                                  tile_position=(0, p0))
                last.then_inc(pe_o, 1)
                pe.wait_ge(oT_ready, gi + 1)
                if gi >= 1:
                    pe.wait_ge(h_ready, gi)
                for k in range(DC):
                    last = mm(ps[0:r, 6, 0:D], oT[:, gi % 2, k, 0:r], wo[:, k, :], start=(k == 0),
                              stop=(k == DC - 1))
                last.then_inc(pe_wo, 1)

            scores(0)
            for gi in range(NG):
                if gi + 1 < NG:
                    scores(gi + 1)
                attend(gi)
                if gi >= 1:
                    pe.wait_ge(hn_nat_ready, gi)
                rows_T(gi, hn_ready, 7, pe_hn)
            pe.wait_ge(hnT_ready, TILES)
            for p in range(2):
                for a in range(2):
                    for k in range(DC):
                        cols = (slice(0, BANK), slice(BANK, TP))[a]
                        last = mm(ps[:, 2 * p + a, 0:cols.stop - cols.start], wqT[:, k, p * 128:(p + 1) * 128],
                                  hnT[:, k, cols],
                                  start=(k == 0), stop=(k == DC - 1))
                last.then_inc(pe_q, 1)

            def sims(j, p):
                if j >= 1:
                    pe.wait_ge(sim_read, 2 * (j - 1) + p + 1)
                mm(ps[:, 6 + p, :], qT[:, p, j * 128:(j + 1) * 128],
                   keysBD[:, p, :, :].rearrange("p h k -> p (h k)"), start=True, stop=True).then_inc(pe_sim, 1)

            pe.wait_ge(qT_ready, 2)
            sims(0, 0)
            sims(0, 1)

            def tokens(k, a):
                if a == 0:
                    return hnT[:, k, 0:BANK]
                return hnT[:, k, BANK:TP].rearrange("p (q t) -> p q t", q=Q)[:, :, 0:valid(TILES - 1)]

            width = (BANK, T - BANK)

            for c in range(IC):
                if c >= 1:
                    pe.wait_ge(gu_done, c)
                for i, w in enumerate((gateT, upT)):
                    for a in range(2):
                        for k in range(DC):
                            last = mm(ps[:, 2 * i + a, 0:width[a]], w[:, k, c * 128:(c + 1) * 128], tokens(k, a),
                                      start=(k == 0), stop=(k == DC - 1))
                last.then_inc(pe_gu, 1)
            pe.wait_ge(gu_done, IC)

            def de_T(e):
                if e % 2 == 0:
                    pe.wait_ge(ld_de[(e // 2) % 2], 16 * (e // 4 + 1))
                if e >= 2:
                    pe.wait_ge(deT_ready, e - 1)
                for k in range(DC):
                    last = tr(ps[:, e % 2, k * 128:(k + 1) * 128], de[:, (e // 2) % 2, e % 2, k * 128:(k + 1) * 128],
                              ident)
                last.then_inc(pe_deT, 1)

            de_T(0)
            for e in range(EX):
                if e + 1 < EX:
                    de_T(e + 1)
                pe.wait_ge(deT_ready, e + 1)
                if e >= 2:
                    pe.wait_ge(sil_ready, e - 1)
                for a in range(2):
                    for k in range(DC):
                        last = mm(ps[:, 2 + 2 * (e % 2) + a, 0:width[a]], deT[:, e % 2, k, :], tokens(k, a),
                                  start=(k == 0), stop=(k == DC - 1))
                last.then_inc(pe_s, 1)
                if e % 6 == 4 and e // 6 + 1 < TILES:
                    sims(e // 6 + 1, 0)
                    sims(e // 6 + 1, 1)
            pe.wait_ge(sil_ready, EX)
            pe.wait_ge(ld_ue, 16 * 4)
            n_p = 0

            def experts(j, lo, hi, n_g):
                v = valid(j)
                acc = ps[0:Q * v, 4 + j % 2, 0:D]
                if lo == 0:
                    pe.wait_ge(g_ready, n_g)
                    if j >= 2:
                        pe.wait_ge(fin_ready, j - 1)
                    for c in range(IC):
                        mm(acc, actT[:, c, j * 128:j * 128 + Q * v], downT[:, c, :], start=(c == 0), stop=False)
                for e in range(lo, hi):
                    last = mm(acc, sil[:, e, j * 128:j * 128 + Q * v], ue[:, e, :], start=False, stop=(e == EX - 1))
                if hi == EX:
                    last.then_inc(pe_out, 1)

            for j in range(TILES):
                pe.wait_ge(slots_ready, 2 * (j + 1))
                n_g, done = n_p, 0
                rounds = -(-valid(j) // ROUND)
                for i in range(rounds):
                    w = min(ROUND, valid(j) - i * ROUND)
                    if n_p >= 1:
                        pe.wait_ge(g_ready, n_p)
                    for t in range(w):
                        tok = (j % RING) * TT + i * ROUND + t
                        for q in range(Q):
                            rows = slice(32 * q, 32 * q + 32)
                            for a in range(2):
                                last = mm(ps[:, q, 32 * t:32 * t + 32], R[rows, tok, :], A[rows, a, tok, :],
                                          start=(a == 0), stop=(a == 1))
                    last.then_inc(pe_p, 1)
                    n_p += 1
                    if j >= 1:
                        hi = EX * (i + 1) // rounds
                        experts(j - 1, done, hi, n_g)
                        done = hi
            experts(TILES - 1, 0, EX, n_p)


def constants():
    import numpy as np
    c = np.zeros((128, C_ALL), np.float32)
    c[:, C_ID:C_ID + 128] = np.eye(128)
    half = DK // 2
    freq = (1.0 / np.float32(10000.0) ** (np.arange(half, dtype=np.float32) / half)).astype(np.float32)
    ang = (np.arange(S, dtype=np.float32)[None, :] * freq[:, None]).astype(np.float32)
    pair = (np.arange(128) % DK) // 2
    c[:, C_COS:C_COS + S] = np.cos(ang)[pair]
    c[:, C_SIN:C_SIN + S] = np.sin(ang)[pair]
    row = np.arange(128) % S
    c[:, C_CAUSAL:C_CAUSAL + S] = np.where(np.arange(S)[None, :] <= row[:, None], 0.0, NEG)
    c[:, C_HEAD:C_HEAD + HP] = np.arange(HP)[None, :] == (np.arange(128) // DK)[:, None]
    c[:, C_PAR:C_PAR + 2 * DK] = (np.arange(2 * DK) // DK)[None, :] == (np.arange(128) // S)[:, None]
    c[:, C_IOTA:C_IOTA + 128] = np.arange(128)[None, :]
    return c


_INS = ["x", "L0_tok_W", "L0_tok_b", "L0_tok_class_token", "L0_tok_pos_emb", "L0_attn_w_qkv", "L0_attn_w_o",
        "L0_ffn_w_queries", "L0_ffn_keys", "L0_ffn_down_embed", "L0_ffn_up_embed", "L0_ffn_w_gate",
        "L0_ffn_w_up", "L0_ffn_w_down"]


def kernel(**inputs):
    import numpy as _np
    import concourse.bacc as _bacc
    from concourse.bass_utils import run_bass_kernel_spmd as _run

    nc = _bacc.Bacc("TRN2", target_bir_lowering=False, num_devices=1)
    arrays, args = {}, []
    for name in _INS:
        a = _np.ascontiguousarray(inputs[name])
        arrays[f"in_{name}"] = a
        args.append(nc.dram_tensor(f"in_{name}", a.shape, mybir.dt.from_np(a.dtype), kind="ExternalInput").ap())
    c = constants()
    arrays["in_consts"] = c
    args.append(nc.dram_tensor("in_consts", c.shape, F32, kind="ExternalInput").ap())
    out = nc.dram_tensor("out_0", (T, D), F32, kind="ExternalOutput").ap()
    vit_tower(nc, *args, out)
    r = _run(nc, [arrays], core_ids=[0])
    return r.results[0]["out_0"].reshape(B, S, D)
```

```python
import concourse.bass as bass
from concourse import mybir
from contextlib import ExitStack

F32 = mybir.dt.float32
F16 = mybir.dt.float16
F32R = mybir.dt.float32r
BF16 = mybir.dt.bfloat16
U32 = mybir.dt.uint32
ALU = mybir.AluOpType
ACT = mybir.ActivationFunctionType
AX = mybir.AxisListType

B, CIN, IMG, PATCH = 16, 3, 96, 16
SIDE = IMG // PATCH
D = 256
S = SIDE * SIDE + 1
T = B * S
KC_TOK = CIN * PATCH * PATCH // 128
DC = D // 128
H, DK = 16, 16
HP = 128 // DK
PER = 111 // S
GROUPS = [(b, min(PER, B - b)) for b in range(0, B, PER)]
ROWS = PER * S
PAIRS = H // 2
FH, NK, FN, TOPK = 4, 128, 32, 8
SLOTS = FH * TOPK
E = 4096
EX = E // NK
INTER = 512
IC = INTER // 128
Q = 4
TQ = T // Q
TQP = 160
TT = 32
TILES = TQP // TT
TP = Q * TQP
BANK = 512
HALF = T // 2
ACT_HEADS = (1, 4, 7)
SEGS = [4, 4, 6, 6, 12]
ROUND = 8
RING = 4
EPS = 1e-5
WSCALE = float(2 ** 14)
NEG = -1e30

C_ID = 0
C_COS = C_ID + 128
C_SIN = C_COS + S
C_CAUSAL = C_SIN + S
C_HEAD = C_CAUSAL + S
C_PAR = C_HEAD + HP
C_IOTA = C_PAR + 2 * DK
C_ALL = C_IOTA + 128


def valid(j):
    return min(TT, TQ - j * TT)


def vit_tower(nc, x, w_tok, b_tok, cls_tok, pos, w_qkv, w_o, w_queries, keys, down_e, up_e,
              w_gate, w_up, w_down, consts, out):
    ctx = ExitStack()
    with ctx:
        def sb(name, shape, dt=F32):
            return ctx.enter_context(nc.sbuf_tensor(name, shape, dt))

        def sem(name):
            return ctx.enter_context(nc.semaphore(name))

        con = sb("con", [128, C_ALL])
        ident = con[:, C_ID:C_ID + 128]
        ident_h = sb("ident_h", [128, 128], BF16)
        ident_r = sb("ident_r", [128, 128], F32R)
        causal_h = sb("causal_h", [128, S], BF16)
        slot_a_words = RING * 2 * Q * EX * ROUND // 2
        w_words = DC * D + 2 * FH * NK + 2 * DC * INTER + 2 * TP
        late = sb("late", [128, max(slot_a_words, w_words)])
        A = late[:, 0:slot_a_words].bitcast(F16).rearrange("p (i a q x t) -> p i a q x t", i=RING, a=2, q=Q, x=EX)
        w_at = [0]

        def late_part(*dims):
            width = dims[0] * dims[1]
            w_at[0] += width
            return late[:, w_at[0] - width:w_at[0]].rearrange("p (a b) -> p a b", a=dims[0])

        wqT = late_part(DC, D)
        keysBD = late_part(2, FH * NK).rearrange("p a (h k) -> p a h k", h=FH)
        gateT = late_part(DC, INTER)
        upT = late_part(DC, INTER)
        qT = late_part(2, TP)
        downT = sb("downT", [128, IC, D])
        ue = sb("ue", [128, EX, D])
        hnT = sb("hnT", [128, DC, TP])
        actT = sb("actT", [128, IC, T])
        de = sb("de", [128, 2, 2, D])
        de_hi = sb("de_hi", [128, 2, 2, D], F32R)
        de_lo = sb("de_lo", [128, 2, 2, D], F32R)
        deT = sb("deT", [128, 3, 2, DC, 128], F32R)
        hn_hi = sb("hn_hi", [128, DC, TP], F32R)
        hn_lo = sb("hn_lo", [128, DC, TP], F32R)
        resid = hnT[:, :, :].rearrange("p k t -> p (k t)").rearrange("p (j d) -> p j d", j=TILES)

        big = sb("big", [128, EX * T])
        sil = big[:, :].rearrange("p (e t) -> p e t", e=EX)
        at = 0

        def part(width):
            nonlocal at
            at += width
            assert at <= EX * T
            return big[:, at - width:at]

        tok_words = CIN * PATCH * IMG + KC_TOK * (T + D)
        early = part(tok_words)
        x_sb = early[:, 0:CIN * PATCH * IMG].rearrange("p (c r w) -> p c r w", c=CIN, r=PATCH)
        patchT = early[:, CIN * PATCH * IMG:tok_words - KC_TOK * D].rearrange("p (k t) -> p k t", k=KC_TOK)
        wtok = early[:, tok_words - KC_TOK * D:tok_words].rearrange("p (k n) -> p k n", k=KC_TOK)
        kexp = early[:, 0:2 * B * HP * S].rearrange("p (a b h s) -> p a b h s", a=2, b=B, h=HP)

        slot_words = max(14 * D, RING * ROUND * 128 // 2)
        slots = sb("slots", [128, slot_words])
        slots_h = slots[:, :].bitcast(F16)
        R = slots_h[:, 0:RING * ROUND * 128].rearrange("p (i y t) -> p i y t", i=RING, y=128)
        nat = slots[:, 0:14 * D].rearrange("p (a n) -> p a n", n=D)
        wq_nat, gate_nat, up_nat = nat[:, 0:2, :], nat[:, 2:6, :], nat[:, 6:10, :]
        down_nat = slots[:, 10 * D:14 * D].rearrange("p (a n) -> p a n", a=2)
        hn_nat = slots[:, 0:DC * T].rearrange("p (k t) -> p k t", k=DC)

        ue_flat = ue[:, :, :].rearrange("p e n -> p (e n)")
        qpad = ue_flat[:, 0:2 * B * ROWS].rearrange("p (a b r) -> p a b r", a=2, b=B)
        vblk = ue_flat[:, 2 * B * ROWS:2 * B * ROWS + B * D].rearrange("p (b c) -> p b c", b=B)
        x_re = ue_flat[:, 2 * B * ROWS:2 * B * ROWS + CIN * PATCH * IMG].rearrange(
            "p (c w n) -> p c w n", c=CIN, w=SIDE)
        xnT = actT[:, :, :].rearrange("p c t -> p (c t)")[:, 0:DC * T].rearrange("p (k t) -> p k t", k=DC)
        wqkv = part(DC * 3 * D).rearrange("p (k n) -> p k n", k=DC)
        wsw = part(DC * 2 * D).rearrange("p (k n) -> p k n", k=DC)
        wo = part(DC * D).rearrange("p (k n) -> p k n", k=DC)
        posful = part(D)
        addend = part(D)
        h = part(len(GROUPS) * D).rearrange("p (g n) -> p g n", n=D)
        keys_nat = part(FH * 2 * FN).rearrange("p (a h n) -> p a h n", h=FH, a=2)
        pr = part(2 * H * S).rearrange("p (g h s) -> p g h s", g=2, h=H)
        pT = part(2 * PAIRS * ROWS).rearrange("p (g c r) -> p g c r", g=2, c=PAIRS)
        vT = big[:, at - 2 * (H * S + PAIRS * ROWS):at - 2 * (H * S + PAIRS * ROWS) + 2 * DC * T].rearrange(
            "p (k b two s) -> p k b two s", k=DC, b=B, two=2)
        oT = part(2 * 2 * ROWS).rearrange("p (g a r) -> p g a r", g=2, a=2)
        xn = sb("xn", [128, 2, D])
        stats = sb("stats", [128, 6])
        mv = sb("mv", [128, 2])
        rs = sb("rs", [128, 4])
        red = sb("red", [128, 3, H])
        top = sb("top", [128, 2, FH, TOPK])
        topi = sb("topi", [128, 2, FH, TOPK], U32)
        topf = sb("topf", [128, 2, FH, TOPK])
        cand = sb("cand", [128, FH, TOPK, TOPK])
        best = sb("best", [128, FH, TOPK])
        besti = sb("besti", [128, FH, TOPK], U32)
        sel = sb("sel", [128, 2, FH, TOPK], U32)
        self_ = sb("self_", [128, 2, FH, TOPK])
        pick = sb("pick", [128, 2, FH, TOPK])
        oneh = sb("oneh", [128, FH, TOPK, TOPK])
        iota_rep = sb("iota_rep", [128, 128, ROUND], F16)
        over = sb("over", [128, FH, TOPK])
        ex = sb("ex", [128, TILES, FH, TOPK])
        den = sb("den", [128, TILES, FH])
        pack = sb("pack", [128, TILES, 4, SLOTS], F16)
        packT = sb("packT", [128, TILES, 4, TT], F16)
        eqx = sb("eqx", [128, EX, ROUND], F16)
        fin = xn
        sg = slots[:, 0:T]
        rot = qT[:, :, 0:T]
        kT = sg[:, :]

        ps = ctx.enter_context(nc.psum_tensor("ps", [128, 8, 512], F32))

        def flat(bank, width):
            return ps[:, bank:bank + 2, :].rearrange("p a c -> p (a c)")[:, 0:width]

        h_dram = nc.dram_tensor("h_scratch", (T, D), F32, kind="Internal").ap()

        ld_con, ld_wtok, ld_pos = sem("ld_con"), sem("ld_wtok"), sem("ld_pos")
        ld_x = [sem(f"ld_x{c}") for c in range(CIN)]
        ld_qkv, ld_wo, ld_nat, ld_ue = sem("ld_qkv"), sem("ld_wo"), sem("ld_nat"), sem("ld_ue")
        ld_de = [sem("ld_de0"), sem("ld_de1")]
        ld_res, st_h = sem("ld_res"), sem("st_h")
        st_out = [sem("st_out0"), sem("st_out1")]
        dve_chain, act_chain, pool_chain = sem("dve_chain"), sem("act_chain"), sem("pool_chain")
        s_const, s_zero = sem("s_const"), sem("s_zero")
        pe_nat, act_nat, re_dve, re_act = sem("pe_nat"), sem("act_nat"), sem("re_dve"), sem("re_act")
        pe_patch, patch_dve, patch_act = sem("pe_patch"), sem("patch_dve"), sem("patch_act")
        pe_emb, xn_ready, pe_xn, xnT_ready = sem("pe_emb"), sem("xn_ready"), sem("pe_xn"), sem("xnT_ready")
        sw_ready, pe_qk, rope_done, kT_ready, kexp_dve, kexp_act = (
            sem("sw_ready"), sem("pe_qk"), sem("rope_done"), sem("kT_ready"), sem("kexp_dve"), sem("kexp_act"))
        pe_vT, vT_ready, pe_v, v_ready = sem("pe_vT"), sem("vT_ready"), sem("pe_v"), sem("v_ready")
        pe_sc, sc_sub, exp_done, prob_ready = sem("pe_sc"), sem("sc_sub"), sem("exp_done"), sem("prob_ready")
        pe_pT, pT_ready, pe_o, oT_ready, pe_wo = (
            sem("pe_pT"), sem("pT_ready"), sem("pe_o"), sem("oT_ready"), sem("pe_wo"))
        hn_ready, pe_hn, hn_nat_ready, hnT_ready, h_ready = (
            sem("hn_ready"), sem("pe_hn"), sem("hn_nat_ready"), sem("hnT_ready"), sem("h_ready"))
        pe_q, qT_ready, pe_sim, sim_read = sem("pe_q"), sem("qT_ready"), sem("pe_sim"), sem("sim_read")
        pe_gate, pe_gu, gate_act, gu_done = (
            sem("pe_gate"), sem("pe_gu"), sem("gate_act"), sem("gu_done"))
        split_ready, hn_hi_ready, hn_lo_ready = sem("split_ready"), sem("hn_hi_ready"), sem("hn_lo_ready")
        pe_deT, deT_ready, pe_s, sil_ready = sem("pe_deT"), sem("deT_ready"), sem("pe_s"), sem("sil_ready")
        lg_ready, lg_exp, slots_ready = sem("lg_ready"), sem("lg_exp"), sem("slots_ready")
        pe_p, g_ready, pe_out, fin_ready = sem("pe_p"), sem("g_ready"), sem("pe_out"), sem("fin_ready")

        NG = len(GROUPS)
        NG_BANKS = 6
        NPOS = 2 * PER

        def load_pixels(queue, c):
            for r in range(SIDE):
                queue.dma_start(x_sb[r * B:(r + 1) * B, c], x[:, c, r * PATCH:(r + 1) * PATCH, :]
                                ).then_inc(ld_x[c], 16)

        block = ctx.enter_context(nc.Block())

        @block.sync
        def _(sp):
            for c in (0, 2):
                load_pixels(sp, c)
            for i in range(PER):
                sp.dma_start(addend[i * S:i * S + 1, :], cls_tok[0, :, :]).then_inc(ld_pos, 16)
                sp.dma_start(addend[i * S + 1:(i + 1) * S, :],
                             b_tok.rearrange("(a n) -> a n", a=1).broadcast_to([S - 1, D])).then_inc(ld_pos, 16)
                sp.dma_start(posful[i * S:(i + 1) * S, :], pos[0, :, :]).then_inc(ld_pos, 16)
            sp.dma_start(wqkv[:, :, :], w_qkv.rearrange("(k p) n -> p k n", p=128)).then_inc(ld_qkv, 16)
            sp.dma_start(wq_nat, w_queries.rearrange("(a p) n -> p a n", p=128)).then_inc(ld_nat, 16)
            sp.dma_start(gate_nat, w_gate.rearrange("(a p) n -> p a n", p=128)).then_inc(ld_nat, 16)
            sp.dma_start(up_nat, w_up.rearrange("(a p) n -> p a n", p=128)).then_inc(ld_nat, 16)
            sp.dma_start(down_nat, w_down.rearrange("(a p) n -> p a n", p=128)).then_inc(ld_nat, 16)
            for p in range(2):
                sp.dma_start(keys_nat[:, p], keys[:, :, p, :].rearrange("h k n -> k h n")).then_inc(ld_nat, 16)
            sp.dma_start(wo[:, :, :], w_o.rearrange("(k p) n -> p k n", p=128)).then_inc(ld_wo, 16)
            for gi, (b0, n) in enumerate(GROUPS):
                sp.wait_ge(h_ready, gi + 1)
                sp.dma_start(h_dram[b0 * S:(b0 + n) * S, :], h[0:n * S, gi, :]).then_inc(st_h, 16)
            sp.wait_ge(pe_wo, NG)
            up_v = up_e.rearrange("(e p) n -> p e n", p=128)
            for c in range(4):
                w = EX // 4
                sp.dma_start(ue[:, c * w:(c + 1) * w, :], up_v[:, c * w:(c + 1) * w, :]).then_inc(ld_ue, 16)
            sp.wait_ge(st_h, 16 * NG)
            sp.wait_ge(pe_s, EX)
            for j in range(TILES):
                v = valid(j)
                for g in range(Q):
                    t0 = g * TQ + j * TT
                    sp.dma_start(resid[g * v:(g + 1) * v, j, :], h_dram[t0:t0 + v, :]).then_inc(ld_res, 16)
            for j in range(TILES):
                v = valid(j)
                sp.wait_ge(fin_ready, j + 1)
                for g in range(Q):
                    t0 = g * TQ + j * TT
                    sp.dma_start(out[t0:t0 + v, :], fin[g * v:(g + 1) * v, j % 2, :]).then_inc(st_out[j % 2], 16)
            for i in range(2):
                sp.wait_ge(st_out[i], 16 * Q * len(range(i, TILES, 2)))

        @block.gpsimd
        def _(pool):
            nc.gpsimd.memset(patchT.rearrange("p k (b s) -> p k b s", s=S)[:, :, :, 0:1], 0.0).then_inc(s_zero, 1)
            nc.gpsimd.memset(qpad, 0.0).then_inc(s_zero, 1)
            nc.gpsimd.memset(keysBD[:, :, :, :], 0.0).then_inc(s_zero, 1)
            nc.gpsimd.memset(hnT[:, :, 4 * 128:TP], 0.0).then_inc(s_zero, 1)
            pool.wait_ge(ld_qkv, 16)
            for k in range(DC):
                pair = wqkv[:, k, 0:2 * D].rearrange("p (c two) -> p c two", two=2)
                twin = wsw[:, k, :].rearrange("p (c two) -> p c two", two=2)
                nc.gpsimd.tensor_scalar(twin[:, :, 0], pair[:, :, 1], -1.0, None, ALU.mult).then_inc(sw_ready, 1)
                nc.gpsimd.tensor_copy(twin[:, :, 1], pair[:, :, 0]).then_inc(sw_ready, 1)
            for e2 in range(EX // 2 + 1):
                if e2 < EX // 2:
                    if e2 >= 2:
                        pool.wait_ge(split_ready, 2 * (e2 - 1))
                    pool.dma_start(de[:, e2 % 2, :, :],
                                   down_e[e2 * 256:(e2 + 1) * 256, :].rearrange("(a p) n -> p a n", p=128)
                                   ).then_inc(ld_de[e2 % 2], 16)
                if e2 == EX // 2 - 1:
                    pool.wait_ge(pe_sim, 2 * TILES)
                    pool.wait_ge(pe_gu, IC)
                    nc.gpsimd.memset(late[:, 0:slot_a_words], 0.0).then_inc(s_zero, 1)
                if e2 >= 1:
                    i = e2 - 1
                    pool.wait_ge(ld_de[i % 2], 16 * (i // 2 + 1))
                    if i >= 2:
                        pool.wait_ge(pe_deT, 2 * (i - 1))
                    nc.gpsimd.tensor_copy(de_hi[:, i % 2], de[:, i % 2]).then_inc(split_ready, 1)
                    pool.wait_ge(split_ready, 2 * i + 1)
                    nc.gpsimd.tensor_tensor(de_lo[:, i % 2], de[:, i % 2], de_hi[:, i % 2].bitcast(F32),
                                            ALU.subtract).then_inc(split_ready, 1)

        @block.scalar
        def _(act):
            act.dma_start(con[:, :], consts[:, :]).then_inc(ld_con, 16)
            load_pixels(act, 1)
            act.dma_start(wtok[:, :, :], w_tok.rearrange("(k p) n -> p k n", p=128)).then_inc(ld_wtok, 16)
            act.wait_ge(ld_con, 16)
            nc.scalar.copy(ident_h[:, :], ident).then_inc(s_const, 1)
            nc.scalar.copy(ident_r[:, :], ident).then_inc(s_const, 1)
            nc.scalar.copy(causal_h[:, :], con[:, C_CAUSAL:C_CAUSAL + S]).then_inc(s_const, 1)
            act.wait_ge(ld_x[CIN - 1], 16 * SIDE)
            for w in range(SIDE):
                nc.scalar.copy(x_re[0:SIDE * B, CIN - 1, w, :].rearrange("p (r n) -> p r n", r=PATCH),
                               x_sb[0:SIDE * B, CIN - 1, :, w * PATCH:(w + 1) * PATCH]).then_inc(re_act, 1)
            act.wait_ge(s_zero, 1)
            for u in range(1, 2 * KC_TOK, 2):
                act.wait_ge(pe_patch, u + 1)
                kc, half = divmod(u, 2)
                dst = patchT[:, kc, :].rearrange("p (b s) -> p b s", s=S)[:, :, 1:]
                dst = dst.rearrange("p b (r c) -> p c r b", c=SIDE)[:, 3 * half:3 * half + 3]
                nc.scalar.copy(dst, ps[:, u % 4, 0:3 * SIDE * B].rearrange("p (c r b) -> p c r b", c=3, b=B)
                               ).then_inc(patch_act, 1)
            nc.scalar.copy(iota_rep[:, :, :], con[:, C_IOTA:C_IOTA + 128].unsqueeze(2).broadcast_to([128, 128, ROUND])
                           ).then_inc(s_const, 1)
            for gi, (b0, n) in enumerate(GROUPS):
                act.wait_ge(pe_xn, gi + 1)
                r = n * S
                nc.scalar.copy(xnT[:, :, b0 * S:b0 * S + r],
                               ps[:, 6 + gi % 2, 0:2 * r].rearrange("p (k t) -> p k t", k=2)).then_inc(xnT_ready, 1)
            for u in range(8):
                act.wait_ge(pe_nat, u + 1)
                src = ps[:, u % 2, :].rearrange("p (a b) -> p a b", a=4)
                if u == 0:
                    dst = wqT[:, :, :].rearrange("p k (a b) -> p (k a) b", a=2)
                elif u < 3:
                    dst = gateT[:, u - 1, :].rearrange("p (a b) -> p a b", a=4)
                elif u < 5:
                    dst = upT[:, u - 3, :].rearrange("p (a b) -> p a b", a=4)
                elif u < 7:
                    dst = downT[:, 2 * (u - 5):2 * (u - 5) + 2, :].rearrange("p k (a b) -> p (k a) b", a=2)
                else:
                    dst = None
                if dst is not None:
                    nc.scalar.copy(dst, src).then_inc(act_nat, 1)
                else:
                    act.wait_ge(s_zero, 3)
                    for hh in range(FH):
                        nc.scalar.copy(keysBD[32 * hh:32 * hh + 32, :, hh, :],
                                       ps[32 * hh:32 * hh + 32, u % 2, 0:256].rearrange("p (a b) -> p a b", a=2)
                                       ).then_inc(act_nat, 1)
            for a in range(2):
                act.wait_ge(kT_ready, a + 1)
                for hh in ACT_HEADS:
                    nc.scalar.mul(kexp[:, a, :, hh, :], kT.rearrange("p (b s) -> p b s", s=S),
                                  con[:, C_HEAD + hh:C_HEAD + hh + 1]).then_inc(kexp_act, 1)
            for c in range(DC):
                act.wait_ge(pe_vT, c + 1)
                src = ps[:, 4 * c:4 * c + 2, 0:HALF].rearrange("p a (b s) -> p a b s", s=S)
                for i in range(2):
                    nc.scalar.copy(vT[:, c, :, i, :].rearrange("p (a b) s -> p a b s", a=2), src
                                   ).then_inc(vT_ready, 1)

            def exponentials(gi):
                r = GROUPS[gi][1] * S
                act.wait_ge(sc_sub, gi + 1)
                nc.scalar.activation(pr[0:r, gi % 2], pr[0:r, gi % 2], ACT.Exp,
                                     scale=DK ** -0.5).then_inc(exp_done, 1)

            def hn_copy(gi):
                b0, n = GROUPS[gi]
                r = n * S
                act.wait_ge(pe_hn, gi + 1)
                nc.scalar.copy(hn_nat[:, :, b0 * S:b0 * S + r],
                               ps[:, 7, 0:2 * r].rearrange("p (k t) -> p k t", k=2)).then_inc(hn_nat_ready, 1)

            exponentials(0)
            exponentials(1)
            for gi, (b0, n) in enumerate(GROUPS):
                r = n * S
                act.wait_ge(pe_pT, gi + 1)
                if gi >= 2:
                    act.wait_ge(pe_o, gi - 1)
                nc.scalar.copy(pT[0:2 * S, gi % 2, :, 0:r].rearrange("p (a c) r -> p a c r", a=2),
                               ps[0:2 * S, 2:4, 0:4 * r].rearrange("p a (c r) -> p a c r", c=4)
                               ).then_inc(pT_ready, 1)
                act.wait_ge(pe_o, gi + 1)
                if gi >= 2:
                    act.wait_ge(pe_wo, gi - 1)
                nc.scalar.copy(oT[:, gi % 2, :, 0:r],
                               ps[:, 4, 0:256].rearrange("p (a r) -> p a r", a=2)[:, :, 0:r]).then_inc(oT_ready, 1)
                if gi >= 1:
                    hn_copy(gi - 1)
                if gi + 2 < NG:
                    exponentials(gi + 2)
            hn_copy(NG - 1)
            act.wait_ge(s_zero, 4)
            act.wait_ge(hn_nat_ready, NG)
            for j in range(TILES):
                v = valid(j)
                nc.scalar.copy(hnT[:, :, j * 128:(j + 1) * 128].rearrange("p k (q t) -> p k q t", q=Q)[:, :, :, 0:v],
                               hn_nat.rearrange("p k (q t) -> p k q t", q=Q)[:, :, :, j * TT:j * TT + v]
                               ).then_inc(hnT_ready, 1)
            act.wait_ge(hnT_ready, TILES)
            nc.scalar.copy(hn_hi[:, :, :], hnT[:, :, :]).then_inc(hn_hi_ready, 1)
            for p in range(2):
                act.wait_ge(pe_q, p + 1)
                nc.scalar.copy(qT[:, p, :], flat(2 * p, TP)).then_inc(qT_ready, 1)

            def deT_copy(e):
                act.wait_ge(pe_deT, e + 1)
                if e >= 3:
                    act.wait_ge(pe_s, e - 2)
                nc.scalar.copy(deT[:, e % 3], ps[:, e % 2, :].bitcast(F32R)
                               .rearrange("p (i k y) -> p i k y", i=2, k=DC)).then_inc(deT_ready, 1)

            e = 0
            deT_copy(0)
            deT_copy(1)
            act.wait_ge(st_h, 16 * NG)
            for j, seg in enumerate(SEGS):
                for i in range(seg):
                    if j == TILES - 1 and i == seg // 2:
                        act.wait_ge(lg_ready, TILES)
                        nc.scalar.activation(ex[:, :, :, :], ex[:, :, :, :], ACT.Exp).then_inc(lg_exp, 1)
                    if e + 2 < EX:
                        deT_copy(e + 2)
                    act.wait_ge(pe_s, e + 1)
                    nc.scalar.activation(sil[:, e, :], flat(2 + 2 * (e % 2), T), ACT.Silu).then_inc(sil_ready, 1)
                    e += 1
                if j < IC:
                    act.wait_ge(pe_gate, j + 1)
                    if j >= 1:
                        act.wait_ge(gu_done, j)
                    nc.scalar.activation(sg[:, :], flat(2, T), ACT.Silu).then_inc(gate_act, 1)

        @block.vector
        def _(dve):
            counts, newest = {}, []

            def chain(ins, then=dve_chain):
                counts[then] = counts.get(then, 0) + 1
                ins.then_inc(then, 1)
                newest[:] = [(then, counts[then])]

            def behind():
                dve.wait_ge(*newest[0])

            def norm(rows, src, dst, then):
                behind()
                chain(nc.vector.bn_stats(stats[0:rows, :], src))
                behind()
                chain(nc.vector.bn_aggr(mv[0:rows, :], stats[0:rows, :]))
                behind()
                v, nhalf, y, a = (rs[0:rows, i:i + 1] for i in range(4))
                bits = rs[:, :].bitcast(mybir.dt.int32)
                chain(nc.vector.tensor_scalar(v, mv[0:rows, 1:2], EPS, None, ALU.add))
                behind()
                chain(nc.vector.tensor_scalar(nhalf, v, -0.5, None, ALU.mult))
                chain(nc.vector.tensor_scalar(bits[0:rows, 3:4], bits[0:rows, 0:1], 1, None,
                                              ALU.logical_shift_right))
                behind()
                chain(nc.vector.tensor_scalar(bits[0:rows, 2:3], bits[0:rows, 3:4], -1.0, float(0x5f3759df),
                                              ALU.mult, ALU.add))
                for _ in range(3):
                    behind()
                    chain(nc.vector.scalar_tensor_tensor(a, y, nhalf, y, ALU.mult, ALU.mult))
                    behind()
                    chain(nc.vector.scalar_tensor_tensor(y, a, 1.5, y, ALU.add, ALU.mult))
                behind()
                chain(nc.vector.tensor_scalar(dst, src, mv[0:rows, 0:1], y,
                                              ALU.subtract, ALU.mult), then)

            for c in range(CIN - 1):
                dve.wait_ge(ld_x[c], 16 * SIDE)
                for w in range(SIDE):
                    chain(nc.vector.tensor_copy(x_re[0:SIDE * B, c, w, :].rearrange("p (r n) -> p r n", r=PATCH),
                                                x_sb[0:SIDE * B, c, :, w * PATCH:(w + 1) * PATCH]), re_dve)
            dve.wait_ge(ld_pos, 16 * 3 * PER)
            chain(nc.vector.tensor_tensor(posful[0:ROWS, :], posful[0:ROWS, :], addend[0:ROWS, :], ALU.add))
            dve.wait_ge(s_zero, 1)
            for u in range(0, 2 * KC_TOK, 2):
                dve.wait_ge(pe_patch, u + 1)
                kc = u // 2
                dst = patchT[:, kc, :].rearrange("p (b s) -> p b s", s=S)[:, :, 1:]
                dst = dst.rearrange("p b (r c) -> p c r b", c=SIDE)[:, 0:3]
                chain(nc.vector.tensor_copy(dst, ps[:, u % 4, 0:3 * SIDE * B]
                                            .rearrange("p (c r b) -> p c r b", c=3, b=B)), patch_dve)
            for gi, (b0, n) in enumerate(GROUPS):
                r = n * S
                dve.wait_ge(pe_emb, gi + 1)
                behind()
                chain(nc.vector.tensor_tensor(h[0:r, gi, :], ps[0:r, (4 + gi) % NG_BANKS, 0:D], posful[0:r, :], ALU.add))
                if gi >= 2:
                    dve.wait_ge(pe_xn, gi - 1)
                norm(r, h[0:r, gi, :], xn[0:r, gi % 2, :], xn_ready)
            cosb = con[:, C_COS:C_COS + S].unsqueeze(1).unsqueeze(1).broadcast_to([128, 2, B // 2, S])
            sinb = con[:, C_SIN:C_SIN + S].unsqueeze(1).unsqueeze(1).broadcast_to([128, 2, B // 2, S])
            for u in range(4):
                half = u % 2
                dve.wait_ge(pe_qk, u + 1)
                k0 = 4 * (u % 2)
                plain = ps[:, k0:k0 + 2, 0:HALF].rearrange("p a (b s) -> p a b s", s=S)
                twin = ps[:, k0 + 2:k0 + 4, 0:HALF].rearrange("p a (b s) -> p a b s", s=S)
                behind()
                chain(nc.vector.tensor_tensor(rot[:, 0, :].rearrange("p (a b s) -> p a b s", a=2, s=S),
                                              plain, cosb, ALU.mult))
                chain(nc.vector.tensor_tensor(rot[:, 1, :].rearrange("p (a b s) -> p a b s", a=2, s=S),
                                              twin, sinb, ALU.mult), rope_done)
                behind()
                if u >= 2:
                    if u == 2:
                        dve.wait_ge(s_zero, 2)
                    nb = B - B % PER
                    v = [rot[:, i, 0:nb * S].rearrange("p (g i s) -> p g i s", i=PER, s=S) for i in (0, 1)]
                    base = qpad[:, half, 0:nb, :].rearrange("p (g i) r -> p g i r", i=PER)
                    for i in range(PER):
                        chain(nc.vector.tensor_tensor(base[:, :, i, i * S:(i + 1) * S], v[0][:, :, i, :],
                                                      v[1][:, :, i, :], ALU.add))
                    chain(nc.vector.tensor_tensor(qpad[:, half, nb:B, 0:S],
                                                  rot[:, 0, nb * S:].rearrange("p (b s) -> p b s", s=S),
                                                  rot[:, 1, nb * S:].rearrange("p (b s) -> p b s", s=S), ALU.add))
                else:
                    if half == 1:
                        dve.wait_ge(kexp_act, len(ACT_HEADS))
                    chain(nc.vector.tensor_tensor(kT, rot[:, 0, :], rot[:, 1, :], ALU.add), kT_ready)
                    behind()
                    for hh in range(HP):
                        if hh in ACT_HEADS:
                            continue
                        chain(nc.vector.tensor_scalar(kexp[:, half, :, hh, :], kT.rearrange("p (b s) -> p b s", s=S),
                                                      con[:, C_HEAD + hh:C_HEAD + hh + 1], None, ALU.mult), kexp_dve)
            par = con[0:2 * S, C_PAR:C_PAR + 2 * DK].unsqueeze(1).broadcast_to([2 * S, 2 * PAIRS, 2 * DK])
            for u in range(B // 2):
                dve.wait_ge(pe_v, u + 1)
                chain(nc.vector.tensor_tensor(
                    vblk[0:2 * S, 2 * u:2 * u + 2, :].rearrange("p b (c d) -> p (b c) d", d=2 * DK),
                    ps[0:2 * S, u % 4, :].rearrange("p (c d) -> p c d", d=2 * DK), par, ALU.mult), v_ready)

            def softmax_front(gi):
                r = GROUPS[gi][1] * S
                dve.wait_ge(pe_sc, gi + 1)
                if gi >= 2:
                    dve.wait_ge(pe_pT, gi - 1)
                sc = ps[0:r, 0:2, 0:HALF].rearrange("p a (h s) -> p a h s", s=S)
                behind()
                chain(nc.vector.tensor_reduce(red[0:r, 0, :].rearrange("p (a h) -> p a h", a=2), sc, AX.X, ALU.max))
                behind()
                chain(nc.vector.tensor_tensor(pr[0:r, gi % 2].rearrange("p (a h) s -> p a h s", a=2), sc,
                                              red[0:r, 0, :].rearrange("p (a h) -> p a h", a=2).unsqueeze(3)
                                              .broadcast_to([r, 2, HP, S]), ALU.subtract), sc_sub)

            def softmax_back(gi):
                r = GROUPS[gi][1] * S
                dve.wait_ge(exp_done, gi + 1)
                behind()
                chain(nc.vector.tensor_reduce(red[0:r, 1, :], pr[0:r, gi % 2], AX.X, ALU.add))
                behind()
                chain(nc.vector.reciprocal(red[0:r, 2, :], red[0:r, 1, :]))
                behind()
                chain(nc.vector.tensor_tensor(pr[0:r, gi % 2], pr[0:r, gi % 2],
                                              red[0:r, 2, :].unsqueeze(2).broadcast_to([r, H, S]), ALU.mult),
                      prob_ready)

            def hidden(gi):
                r = GROUPS[gi][1] * S
                dve.wait_ge(pe_wo, gi + 1)
                behind()
                chain(nc.vector.tensor_tensor(h[0:r, gi, :], ps[0:r, 5 + gi % 2, 0:D], h[0:r, gi, :], ALU.add), h_ready)
                if gi >= 2:
                    dve.wait_ge(pe_hn, gi - 1)
                norm(r, h[0:r, gi, :], xn[0:r, gi % 2, :], hn_ready)

            softmax_front(0)
            softmax_front(1)
            softmax_back(0)
            for gi in range(1, NG):
                softmax_back(gi)
                if gi + 1 < NG:
                    softmax_front(gi + 1)
                hidden(gi - 1)
            hidden(NG - 1)
            dve.wait_ge(hn_hi_ready, 1)
            chain(nc.vector.tensor_tensor(hn_lo[:, :, :], hnT[:, :, :], hn_hi[:, :, :].bitcast(F32), ALU.subtract),
                  hn_lo_ready)

            iota8 = con[:, C_IOTA:C_IOTA + TOPK]

            rounds = [(j, t0, min(ROUND, valid(j) - t0)) for j in range(TILES) for t0 in range(0, valid(j), ROUND)]

            def build_slots(i):
                j, t0, w = rounds[i]
                if i == 0:
                    dve.wait_ge(s_zero, 5)
                if i >= RING:
                    dve.wait_ge(pe_p, i - RING + 1)
                s_i = i % RING
                behind()
                chain(nc.vector.tensor_tensor(R[:, s_i, :, 0:w], iota_rep[:, :, 0:w],
                                              packT[:, j, 1, t0:t0 + w].unsqueeze(1).broadcast_to([128, 128, w]),
                                              ALU.is_equal))
                chain(nc.vector.tensor_tensor(eqx[:, :, 0:w], iota_rep[:, 0:EX, 0:w],
                                              packT[:, j, 0, t0:t0 + w].unsqueeze(1).broadcast_to([128, EX, w]),
                                              ALU.is_equal))
                behind()
                for q in range(Q):
                    own = slice(SLOTS * q, SLOTS * (q + 1))
                    chain(nc.vector.tensor_tensor(
                        A[own, s_i, :, q, :, 0:w], eqx[own, :, 0:w].unsqueeze(1).broadcast_to([SLOTS, 2, EX, w]),
                        packT[own, j, 2:4, t0:t0 + w].unsqueeze(2).broadcast_to([SLOTS, 2, EX, w]),
                        ALU.mult), slots_ready)

            for j in range(TILES):
                for p in range(2):
                    dve.wait_ge(pe_sim, 2 * j + p + 1)
                    simv = ps[:, 6 + p, :].rearrange("p (h k) -> p h k", h=FH)
                    behind()
                    for hh in range(FH):
                        chain(nc.vector.max(top[:, p, hh, :], simv[:, hh, :]))
                    behind()
                    for hh in range(FH):
                        chain(nc.vector.max_index(topi[:, p, hh, :], top[:, p, hh, :], simv[:, hh, :]),
                              sim_read if hh == FH - 1 else dve_chain)
                behind()
                chain(nc.vector.tensor_copy(topf[:, :, :, :], topi[:, :, :, :]))
                chain(nc.vector.tensor_tensor(cand[:, :, :, :],
                                              top[:, 0].unsqueeze(3).broadcast_to([128, FH, TOPK, TOPK]),
                                              top[:, 1].unsqueeze(2).broadcast_to([128, FH, TOPK, TOPK]), ALU.add))
                behind()
                cf = cand[:, :, :, :].rearrange("p h i j -> p h (i j)")
                for hh in range(FH):
                    chain(nc.vector.max(best[:, hh, :], cf[:, hh, :]))
                behind()
                for hh in range(FH):
                    chain(nc.vector.max_index(besti[:, hh, :], best[:, hh, :], cf[:, hh, :]))
                chain(nc.vector.tensor_tensor(ex[:, j], best[:, :, :],
                                              best[:, :, 0:1].broadcast_to([128, FH, TOPK]), ALU.subtract), lg_ready)
                behind()
                chain(nc.vector.tensor_scalar(sel[:, 0], besti[:, :, :], 3, None, ALU.logical_shift_right))
                chain(nc.vector.tensor_scalar(sel[:, 1], besti[:, :, :], TOPK - 1, None, ALU.bitwise_and))
                behind()
                chain(nc.vector.tensor_copy(self_[:, :, :, :], sel[:, :, :, :]))
                for p in range(2):
                    behind()
                    chain(nc.vector.tensor_tensor(oneh[:, :, :, :],
                                                  self_[:, p].unsqueeze(3).broadcast_to([128, FH, TOPK, TOPK]),
                                                  iota8.unsqueeze(1).unsqueeze(1).broadcast_to([128, FH, TOPK, TOPK]),
                                                  ALU.is_equal))
                    behind()
                    chain(nc.vector.tensor_tensor(oneh[:, :, :, :], oneh[:, :, :, :],
                                                  topf[:, p].unsqueeze(2).broadcast_to([128, FH, TOPK, TOPK]),
                                                  ALU.mult))
                    behind()
                    chain(nc.vector.tensor_reduce(pick[:, p], oneh[:, :, :, :], AX.X, ALU.add))
                behind()
                chain(nc.vector.tensor_scalar(over[:, :, :], pick[:, 0], float(EX), float(NK - 1), ALU.is_ge, ALU.mult))
                chain(nc.vector.tensor_scalar(pack[:, j, 0, :].rearrange("p (h k) -> p h k", h=FH), pick[:, 0],
                                              float(EX - 1), None, ALU.min))
                behind()
                chain(nc.vector.tensor_tensor(pack[:, j, 1, :].rearrange("p (h k) -> p h k", h=FH), pick[:, 1],
                                              over[:, :, :], ALU.max))
                if j < IC:
                    dve.wait_ge(gate_act, j + 1)
                    dve.wait_ge(pe_gu, j + 1)
                    chain(nc.vector.scalar_tensor_tensor(actT[:, j, :], sg[:, :], WSCALE, flat(4, T), ALU.mult,
                                                         ALU.mult), gu_done)
            dve.wait_ge(lg_exp, 1)
            exf = ex[:, :, :, :].rearrange("p j h k -> p (j h) k")
            denf = den[:, :, :].rearrange("p j h -> p (j h)")
            chain(nc.vector.tensor_reduce(denf, exf, AX.X, ALU.add))
            behind()
            chain(nc.vector.reciprocal(denf, denf))
            behind()
            chain(nc.vector.scalar_tensor_tensor(exf, exf, WSCALE,
                                                 denf.unsqueeze(2).broadcast_to([128, TILES * FH, TOPK]),
                                                 ALU.mult, ALU.mult))
            behind()
            wj = ex[:, :, :, :].rearrange("p j h k -> p j (h k)")
            chain(nc.vector.tensor_copy(pack[:, :, 2, :], wj))
            behind()
            chain(nc.vector.tensor_tensor(pack[:, :, 3, :], wj, pack[:, :, 2, :], ALU.subtract))
            behind()
            chain(nc.vector.transpose(packT[:, :, :, :].rearrange("p j a t -> p (j a t)"),
                                      pack[:, :, :, :].rearrange("p j a s -> p (j a s)")))
            for i in range(RING):
                build_slots(i)
            dve.wait_ge(sil_ready, EX)
            n_p = 0

            def finish(j):
                v = valid(j)
                dve.wait_ge(pe_out, j + 1)
                if j == 0:
                    dve.wait_ge(ld_res, 16 * Q * TILES)
                if j >= 2:
                    dve.wait_ge(st_out[j % 2], 16 * Q * (j // 2))
                chain(nc.vector.scalar_tensor_tensor(fin[0:Q * v, j % 2, :], ps[0:Q * v, 4 + j % 2, 0:D],
                                                     1.0 / WSCALE, resid[0:Q * v, j, :], ALU.mult, ALU.add),
                      fin_ready)

            for i, (j, t0, w) in enumerate(rounds):
                dve.wait_ge(pe_p, i + 1)
                pv = flat(2 * (i % 2), Q * EX * w).rearrange("p (t q e) -> p q e t", e=EX, q=Q)
                dst = sil[:, :, j * 128:j * 128 + Q * valid(j)].rearrange("p e (q t) -> p q e t", q=Q)
                dst = dst[:, :, :, t0:t0 + w]
                behind()
                chain(nc.vector.tensor_tensor(dst, pv, dst, ALU.mult), g_ready)
                if i + RING < len(rounds):
                    build_slots(i + RING)
                if t0 + w == valid(j) and j >= 1:
                    finish(j - 1)
            finish(TILES - 1)

        @block.tensor
        def _(pe):
            mm, tr = nc.tensor.matmul, nc.tensor.transpose
            pe.wait_ge(ld_con, 16)
            for u in range(2 * KC_TOK):
                kc, half = divmod(u, 2)
                c, px = kc // 2, slice(128 * (kc % 2), 128 * (kc % 2) + 128)
                if kc % 2 == 0 and half == 0:
                    if c < CIN - 1:
                        pe.wait_ge(re_dve, SIDE * (c + 1))
                    else:
                        pe.wait_ge(re_act, SIDE)
                if u >= 4:
                    pe.wait_ge((patch_dve, patch_act)[u % 2], u // 2 - 1)
                for wp in range(3):
                    last = tr(ps[:, u % 4, wp * SIDE * B:(wp + 1) * SIDE * B],
                              x_re[0:SIDE * B, c, 3 * half + wp, px], ident[0:SIDE * B, 0:SIDE * B])
                last.then_inc(pe_patch, 1)
            pe.wait_ge(patch_dve, KC_TOK)
            pe.wait_ge(patch_act, KC_TOK)
            pe.wait_ge(ld_wtok, 16)

            def rows_T(gi, ready, bank, done):
                r = GROUPS[gi][1] * S
                pe.wait_ge(ready, gi + 1)
                for k in range(DC):
                    last = tr(ps[:, bank, k * r:(k + 1) * r], xn[0:r, gi % 2, k * 128:(k + 1) * 128],
                              ident[0:r, 0:r])
                last.then_inc(done, 1)

            for gi, (b0, n) in enumerate(GROUPS):
                r = n * S
                for k in range(KC_TOK):
                    last = mm(ps[0:r, (4 + gi) % NG_BANKS, 0:D], patchT[:, k, b0 * S:b0 * S + r], wtok[:, k, :],
                              start=(k == 0), stop=(k == KC_TOK - 1))
                last.then_inc(pe_emb, 1)
                if gi >= 1:
                    if gi >= 3:
                        pe.wait_ge(xnT_ready, gi - 2)
                    rows_T(gi - 1, xn_ready, 6 + (gi - 1) % 2, pe_xn)
            pe.wait_ge(xnT_ready, NG - 2)
            rows_T(NG - 1, xn_ready, 6 + (NG - 1) % 2, pe_xn)
            pe.wait_ge(ld_nat, 16 * 6)
            blocks = []
            blocks.append([wq_nat[:, a, k * 128:(k + 1) * 128] for k in range(2) for a in range(2)])
            for src in (gate_nat, up_nat):
                for k in range(2):
                    blocks.append([src[:, a, k * 128:(k + 1) * 128] for a in range(4)])
            for k2 in range(2):
                blocks.append([down_nat[:, a, k * 128:(k + 1) * 128] for k in (2 * k2, 2 * k2 + 1) for a in range(2)])
            blocks.append([keys_nat[:, p].rearrange("p h n -> p (h n)") for p in range(2)])
            for u, bl in enumerate(blocks):
                if u >= 2:
                    pe.wait_ge(act_nat, u - 1)
                for i, src in enumerate(bl):
                    last = tr(ps[:, u % 2, i * 128:(i + 1) * 128], src, ident)
                last.then_inc(pe_nat, 3 if u == len(blocks) - 1 else 1)
            pe.wait_ge(xnT_ready, NG)
            pe.wait_ge(sw_ready, 2 * DC)
            pe.wait_ge(act_nat, 7 + FH)
            for u in range(4):
                if u >= 2:
                    pe.wait_ge(rope_done, u - 1)
                for i, w in enumerate((wqkv, wsw)):
                    for a in range(2):
                        for k in range(DC):
                            c = (u + 2) % 4
                            last = mm(ps[:, 4 * (u % 2) + 2 * i + a, 0:HALF], w[:, k, c * 128:(c + 1) * 128],
                                      xnT[:, k, a * HALF:(a + 1) * HALF], start=(k == 0), stop=(k == DC - 1))
                last.then_inc(pe_qk, 1)
            for c in range(DC):
                pe.wait_ge(rope_done, 3 + c)
                for a in range(2):
                    for k in range(DC):
                        last = mm(ps[:, 4 * c + a, 0:HALF], wqkv[:, k, 2 * D + c * 128:2 * D + (c + 1) * 128],
                                  xnT[:, k, a * HALF:(a + 1) * HALF], start=(k == 0), stop=(k == DC - 1))
                last.then_inc(pe_vT, 1)
            pe.wait_ge(vT_ready, 4)
            for u in range(B // 2):
                if u >= 4:
                    pe.wait_ge(v_ready, u - 3)
                for i in range(2):
                    b = 2 * u + i
                    for c in range(DC):
                        last = tr(ps[0:2 * S, u % 4, i * D + c * 128:i * D + (c + 1) * 128],
                                  vT[:, c, b, :, :].rearrange("p two s -> p (two s)"), ident)
                last.then_inc(pe_v, 1)
            pe.wait_ge(v_ready, B // 2)
            pe.wait_ge(kexp_dve, 2 * (HP - len(ACT_HEADS)))
            pe.wait_ge(kexp_act, 2 * len(ACT_HEADS))
            pe.wait_ge(s_const, 4)
            pe.wait_ge(ld_wo, 16)

            def scores(gi, a):
                b0, n = GROUPS[gi]
                r = n * S
                if gi >= 1 and a == 0:
                    pe.wait_ge(sc_sub, gi)
                bank = a
                mm(ps[0:r, bank, 0:HALF], ident_h[0:r, 0:r],
                   causal_h[0:r, :].unsqueeze(1).broadcast_to([r, HP, S]), start=True, stop=False)
                for i in range(n):
                    last = mm(ps[0:r, bank, 0:HALF], qpad[:, a, b0 + i, 0:r],
                              kexp[:, a, b0 + i].rearrange("p h s -> p (h s)"), start=False, stop=(i == n - 1))
                if a == 1:
                    last.then_inc(pe_sc, 1)

            def probs_T(gi):
                r = GROUPS[gi][1] * S
                pe.wait_ge(prob_ready, gi + 1)
                if gi >= 1:
                    pe.wait_ge(pT_ready, gi)
                for c in range(PAIRS):
                    last = tr(ps[0:2 * S, 2 + c // 4, (c % 4) * r:(c % 4 + 1) * r],
                              pr[0:r, gi % 2, 2 * c:2 * c + 2, :].rearrange("p h s -> p (h s)"), ident[0:r, 0:r])
                last.then_inc(pe_pT, 1)

            def attend(gi):
                b0, n = GROUPS[gi]
                pe.wait_ge(pT_ready, gi + 1)
                if gi >= 1:
                    pe.wait_ge(oT_ready, gi)
                for i in range(n):
                    for c in range(PAIRS):
                        p0 = 32 * (c % 4)
                        col = 128 * (c // 4) + i * S
                        last = mm(ps[p0:p0 + 32, 4, col:col + S],
                                  vblk[0:2 * S, b0 + i, 32 * c:32 * c + 32],
                                  pT[0:2 * S, gi % 2, c, i * S:(i + 1) * S], start=True, stop=True,
                                  tile_position=(0, p0))
                last.then_inc(pe_o, 1)

            def project(gi):
                r = GROUPS[gi][1] * S
                pe.wait_ge(oT_ready, gi + 1)
                if gi >= 2:
                    pe.wait_ge(h_ready, gi - 1)
                for k in range(DC):
                    last = mm(ps[0:r, 5 + gi % 2, 0:D], oT[:, gi % 2, k, 0:r], wo[:, k, :], start=(k == 0),
                              stop=(k == DC - 1))
                last.then_inc(pe_wo, 1)

            for gi in range(2):
                for a in range(2):
                    scores(gi, a)
            for gi in range(NG):
                probs_T(gi)
                if gi + 2 < NG:
                    scores(gi + 2, 0)
                attend(gi)
                if gi + 2 < NG:
                    scores(gi + 2, 1)
                project(gi)
                if gi >= 1:
                    if gi >= 2:
                        pe.wait_ge(hn_nat_ready, gi - 1)
                    rows_T(gi - 1, hn_ready, 7, pe_hn)
            pe.wait_ge(hn_nat_ready, NG - 1)
            rows_T(NG - 1, hn_ready, 7, pe_hn)
            pe.wait_ge(hnT_ready, TILES)
            for p in range(2):
                for a in range(2):
                    for k in range(DC):
                        cols = (slice(0, BANK), slice(BANK, TP))[a]
                        last = mm(ps[:, 2 * p + a, 0:cols.stop - cols.start], wqT[:, k, p * 128:(p + 1) * 128],
                                  hnT[:, k, cols],
                                  start=(k == 0), stop=(k == DC - 1))
                last.then_inc(pe_q, 1)

            def sims(j, p):
                if j >= 1:
                    pe.wait_ge(sim_read, 2 * (j - 1) + p + 1)
                mm(ps[:, 6 + p, :], qT[:, p, j * 128:(j + 1) * 128],
                   keysBD[:, p, :, :].rearrange("p h k -> p (h k)"), start=True, stop=True).then_inc(pe_sim, 1)

            pe.wait_ge(qT_ready, 2)
            sims(0, 0)
            sims(0, 1)

            def tokens(src, k, a):
                if a == 0:
                    return src[:, k, 0:BANK]
                return src[:, k, BANK:TP].rearrange("p (q t) -> p q t", q=Q)[:, :, 0:valid(TILES - 1)]

            width = (BANK, T - BANK)

            def gated(bank, w, c, done):
                for a in range(2):
                    for k in range(DC):
                        last = mm(ps[:, bank + a, 0:width[a]], w[:, k, c * 128:(c + 1) * 128], tokens(hnT, k, a),
                                  start=(k == 0), stop=(k == DC - 1))
                last.then_inc(done, 1)

            def de_T(e):
                i = (e // 2) % 2
                if e % 2 == 0:
                    pe.wait_ge(split_ready, 2 * (e // 2 + 1))
                if e >= 2:
                    pe.wait_ge(deT_ready, e - 1)
                for n, src in enumerate((de_hi, de_lo)):
                    for k in range(DC):
                        last = tr(ps[:, e % 2, (2 * n + k) * 128:(2 * n + k + 1) * 128].bitcast(F32R),
                                  src[:, i, e % 2, k * 128:(k + 1) * 128], ident_r[:, :])
                last.then_inc(pe_deT, 1)

            pe.wait_ge(hn_hi_ready, 1)
            pe.wait_ge(hn_lo_ready, 1)
            e = 0
            de_T(0)
            de_T(1)
            for j, seg in enumerate(SEGS):
                for _ in range(seg):
                    if e + 2 < EX:
                        de_T(e + 2)
                    pe.wait_ge(deT_ready, e + 1)
                    if e >= 2:
                        pe.wait_ge(sil_ready, e - 1)
                    for a in range(2):
                        parts = [(i, src, k) for k in range(DC) for i, src in ((0, hn_hi), (0, hn_lo), (1, hn_hi))]
                        for n, (i, src, k) in enumerate(parts):
                            last = mm(ps[:, 2 + 2 * (e % 2) + a, 0:width[a]], deT[:, e % 3, i, k, :],
                                      tokens(src, k, a), start=(n == 0), stop=(n == len(parts) - 1))
                    last.then_inc(pe_s, 1)
                    e += 1
                if j < IC:
                    pe.wait_ge(sil_ready, e - 1)
                    gated(2, gateT, j, pe_gate)
                    pe.wait_ge(sil_ready, e)
                    gated(4, upT, j, pe_gu)
                if j + 1 < TILES:
                    sims(j + 1, 0)
                    sims(j + 1, 1)
                if j < IC:
                    pe.wait_ge(gate_act, j + 1)
                    pe.wait_ge(gu_done, j + 1)
            pe.wait_ge(sil_ready, EX)
            pe.wait_ge(ld_ue, 16 * 4)
            n_p = 0

            def experts(j, lo, hi, n_g):
                v = valid(j)
                acc = ps[0:Q * v, 4 + j % 2, 0:D]
                if lo == 0:
                    if j >= 2:
                        pe.wait_ge(fin_ready, j - 1)
                    for c in range(IC):
                        mm(acc, actT[:, c, j * 128:j * 128 + Q * v], downT[:, c, :], start=(c == 0), stop=False)
                    pe.wait_ge(g_ready, n_g)
                for e in range(lo, hi):
                    last = mm(acc, sil[:, e, j * 128:j * 128 + Q * v], ue[:, e, :], start=False, stop=(e == EX - 1))
                if hi == EX:
                    last.then_inc(pe_out, 1)

            for j in range(TILES):
                n_g, done = n_p, 0
                rounds = -(-valid(j) // ROUND)
                for i in range(rounds):
                    w = min(ROUND, valid(j) - i * ROUND)
                    pe.wait_ge(slots_ready, Q * (n_p + 1))
                    if n_p >= 2:
                        pe.wait_ge(g_ready, n_p - 1)
                    for t in range(w):
                        dense = flat(2 * (n_p % 2), 2 * BANK)[:, Q * EX * t:Q * EX * (t + 1)]
                        for a in range(2):
                            last = mm(dense, R[:, n_p % RING, :, t],
                                      A[:, n_p % RING, a, :, :, t].rearrange("p q x -> p (q x)"),
                                      start=(a == 0), stop=(a == 1))
                    last.then_inc(pe_p, 1)
                    n_p += 1
                    if j >= 1:
                        hi = EX * (i + 1) // rounds
                        experts(j - 1, done, hi, n_g)
                        done = hi
            experts(TILES - 1, 0, EX, n_p)


def constants():
    import numpy as np
    c = np.zeros((128, C_ALL), np.float32)
    c[:, C_ID:C_ID + 128] = np.eye(128)
    half = DK // 2
    freq = (1.0 / np.float32(10000.0) ** (np.arange(half, dtype=np.float32) / half)).astype(np.float32)
    ang = (np.arange(S, dtype=np.float32)[None, :] * freq[:, None]).astype(np.float32)
    pair = (np.arange(128) % DK) // 2
    c[:, C_COS:C_COS + S] = np.cos(ang)[pair]
    c[:, C_SIN:C_SIN + S] = np.sin(ang)[pair]
    row = np.arange(128) % S
    c[:, C_CAUSAL:C_CAUSAL + S] = np.where(np.arange(S)[None, :] <= row[:, None], 0.0, NEG)
    c[:, C_HEAD:C_HEAD + HP] = np.arange(HP)[None, :] == (np.arange(128) // DK)[:, None]
    c[:, C_PAR:C_PAR + 2 * DK] = (np.arange(2 * DK) // DK)[None, :] == (np.arange(128) // S)[:, None]
    c[:, C_IOTA:C_IOTA + 128] = np.arange(128)[None, :]
    return c


_INS = ["x", "L0_tok_W", "L0_tok_b", "L0_tok_class_token", "L0_tok_pos_emb", "L0_attn_w_qkv", "L0_attn_w_o",
        "L0_ffn_w_queries", "L0_ffn_keys", "L0_ffn_down_embed", "L0_ffn_up_embed", "L0_ffn_w_gate",
        "L0_ffn_w_up", "L0_ffn_w_down"]


def kernel(**inputs):
    import numpy as _np
    import concourse.bacc as _bacc
    from concourse.bass_utils import run_bass_kernel_spmd as _run

    nc = _bacc.Bacc("TRN2", target_bir_lowering=False, num_devices=1)
    arrays, args = {}, []
    for name in _INS:
        a = _np.ascontiguousarray(inputs[name])
        arrays[f"in_{name}"] = a
        args.append(nc.dram_tensor(f"in_{name}", a.shape, mybir.dt.from_np(a.dtype), kind="ExternalInput").ap())
    c = constants()
    arrays["in_consts"] = c
    args.append(nc.dram_tensor("in_consts", c.shape, F32, kind="ExternalInput").ap())
    out = nc.dram_tensor("out_0", (T, D), F32, kind="ExternalOutput").ap()
    vit_tower(nc, *args, out)
    r = _run(nc, [arrays], core_ids=[0])
    return r.results[0]["out_0"].reshape(B, S, D)
```

```python
import concourse.bass as bass
from concourse import mybir
from contextlib import ExitStack

F32 = mybir.dt.float32
F16 = mybir.dt.float16
F32R = mybir.dt.float32r
BF16 = mybir.dt.bfloat16
U32 = mybir.dt.uint32
ALU = mybir.AluOpType
ACT = mybir.ActivationFunctionType
AX = mybir.AxisListType

B, CIN, IMG, PATCH = 16, 3, 96, 16
SIDE = IMG // PATCH
D = 256
S = SIDE * SIDE + 1
T = B * S
KC_TOK = CIN * PATCH * PATCH // 128
DC = D // 128
H, DK = 16, 16
HP = 128 // DK
PER = 111 // S
GROUPS = [(b, min(PER, B - b)) for b in range(0, B, PER)]
ROWS = PER * S
FULL = B // PER
LEFT = B - FULL * PER
PAIRS = H // 2
FH, NK, FN, TOPK = 4, 128, 32, 8
SLOTS = FH * TOPK
E = 4096
EX = E // NK
INTER = 512
IC = INTER // 128
Q = 4
TT = 32
TILES = -(-T // 128)
TP = TILES * 128
BANK = 512
HALF = T // 2
ACT_HEADS = (1, 3)
POOL_HEADS = (0, 2, 4)
SEGS = [4, 4, 4, 4, 16]
ROUND = 8
RING = 4
EPS = 1e-5
WSCALE = float(2 ** 14)
NEG = -1e30

C_ID = 0
C_COS = C_ID + 128
C_SIN = C_COS + S
C_CAUSAL = C_SIN + S
C_HEAD = C_CAUSAL + S
C_PAR = C_HEAD + HP
C_IOTA = C_PAR + 2 * DK
C_ALL = C_IOTA + 128


def valid(j):
    return min(TT, (T - j * 128) // Q)




def vit_tower(nc, x, w_tok, b_tok, cls_tok, pos, w_qkv, w_o, w_queries, keys, down_e, up_e,
              w_gate, w_up, w_down, consts, out):
    ctx = ExitStack()
    with ctx:
        def sb(name, shape, dt=F32):
            return ctx.enter_context(nc.sbuf_tensor(name, shape, dt))

        def sem(name):
            return ctx.enter_context(nc.semaphore(name))

        con = sb("con", [128, C_ALL])
        ident = con[:, C_ID:C_ID + 128]
        ident_h = sb("ident_h", [128, 128], BF16)
        ident_r = sb("ident_r", [128, 128], F32R)
        causal_h = sb("causal_h", [128, S], BF16)
        slot_a_words = RING * 2 * Q * EX * ROUND // 2
        w_words = DC * D + 2 * FH * NK + 2 * TP
        late = sb("late", [128, max(slot_a_words, w_words)])
        A = late[:, 0:slot_a_words].bitcast(F16).rearrange("p (i a q x t) -> p i a q x t", i=RING, a=2, q=Q, x=EX)
        w_at = [0]

        def late_part(*dims):
            width = dims[0] * dims[1]
            w_at[0] += width
            return late[:, w_at[0] - width:w_at[0]].rearrange("p (a b) -> p a b", a=dims[0])

        wqT = late_part(DC, D)
        keysBD = late_part(2, FH * NK).rearrange("p a (h k) -> p a h k", h=FH)
        qT = late_part(2, TP)
        downT = sb("downT", [128, IC, D])
        ue = sb("ue", [128, EX, D])
        rows = sb("rows", [128, TILES * D])
        hnT = rows[:, 0:DC * T].rearrange("p (k t) -> p k t", k=DC)
        resid = rows[:, :].rearrange("p (j d) -> p j d", j=TILES)
        actT = sb("actT", [128, IC, T])
        de = sb("de", [128, 2, 2, D])
        de_hi = sb("de_hi", [128, 2, 2, D], F32R)
        de_lo = sb("de_lo", [128, 2, 2, D], F32R)
        deT = sb("deT", [128, 4, 2, DC, 128], F32R)
        gate_hi = sb("gate_hi", [128, DC, INTER], F32R)
        gate_lo = sb("gate_lo", [128, DC, INTER], F32R)
        hn_hi = sb("hn_hi", [128, DC, T], F32R)
        hn_lo = sb("hn_lo", [128, DC, T], F32R)

        big = sb("big", [128, EX * T])
        sil = big[:, :].rearrange("p (e t) -> p e t", e=EX)
        at = 0

        def part(width):
            nonlocal at
            at += width
            assert at <= EX * T
            return big[:, at - width:at]

        tok_words = CIN * PATCH * IMG + KC_TOK * (T + D)
        early = part(tok_words)
        x_sb = early[:, 0:CIN * PATCH * IMG].rearrange("p (c r w) -> p c r w", c=CIN, r=PATCH)
        patchT = early[:, CIN * PATCH * IMG:tok_words - KC_TOK * D].rearrange("p (k t) -> p k t", k=KC_TOK)
        wtok = early[:, tok_words - KC_TOK * D:tok_words].rearrange("p (k n) -> p k n", k=KC_TOK)
        kexp = early[:, 0:2 * B * HP * S].rearrange("p (a b h s) -> p a b h s", a=2, b=B, h=HP)

        slot_words = max(14 * D, RING * ROUND * 128 // 2)
        slots_base = nc.sbuf_base
        slots = sb("slots", [128, slot_words])
        slots_h = slots[:, :].bitcast(F16)
        R = slots_h[:, 0:RING * ROUND * 128].rearrange("p (i y t) -> p i y t", i=RING, y=128)
        nat = slots[:, 0:14 * D].rearrange("p (a n) -> p a n", n=D)
        wq_nat, gate_nat, up_nat = nat[:, 0:2, :], nat[:, 2:6, :], nat[:, 6:10, :]
        up_hi = nc.alloc_sbuf_tensor_at("up_hi", [128, DC, INTER], F32R, offset=slots_base + 4 * 2 * D)
        up_lo = nc.alloc_sbuf_tensor_at("up_lo", [128, DC, INTER], F32R, offset=slots_base + 4 * 10 * D)
        down_nat = slots[:, 10 * D:14 * D].rearrange("p (a n) -> p a n", a=2)

        vT = slots[:, DC * T:3 * DC * T].rearrange("p (k b two s) -> p k b two s", k=DC, b=B, two=2)

        ue_flat = ue[:, :, :].rearrange("p e n -> p (e n)")
        qpad = ue_flat[:, 0:2 * PER * (FULL * ROWS + S)].rearrange("p (a x) -> p a x", a=2)
        vblk = ue_flat[:, 2 * PER * (FULL * ROWS + S):2 * PER * (FULL * ROWS + S) + B * D].rearrange("p (b c) -> p b c", b=B)
        x_re = ue_flat[:, 2 * PER * (FULL * ROWS + S):2 * PER * (FULL * ROWS + S) + CIN * PATCH * IMG].rearrange(
            "p (c w n) -> p c w n", c=CIN, w=SIDE)
        xnT = actT[:, :, :].rearrange("p c t -> p (c t)")[:, 0:DC * T].rearrange("p (k t) -> p k t", k=DC)
        wqkv = part(DC * 3 * D).rearrange("p (k n) -> p k n", k=DC)
        q_left = part(2 * LEFT * S).rearrange("p (a s) -> p a s", a=2)
        wo = part(DC * D).rearrange("p (k n) -> p k n", k=DC)
        posful = part(D)
        addend = part(D)
        h = part(len(GROUPS) * D).rearrange("p (g n) -> p g n", n=D)
        keys_nat = part(FH * 2 * FN).rearrange("p (a h n) -> p a h n", h=FH, a=2)
        pr = part(2 * H * S).rearrange("p (g h s) -> p g h s", g=2, h=H)
        pT = part(2 * PAIRS * ROWS).rearrange("p (g c r) -> p g c r", g=2, c=PAIRS)
        rot_at = at - 2 * H * S - 2 * PAIRS * ROWS
        rot = big[:, rot_at:rot_at + 4 * T].rearrange("p (i t) -> p i t", i=4)
        oT = part(2 * 2 * ROWS).rearrange("p (g a r) -> p g a r", g=2, a=2)
        xn = sb("xn", [128, 2, D])
        stats = sb("stats", [128, 6])
        mv = sb("mv", [128, 2])
        rs = sb("rs", [128, 1])
        veps, nhalf = sb("veps", [128, 1]), sb("nhalf", [128, 1])
        red = sb("red", [128, 3, H])
        top = sb("top", [128, 2, FH, TOPK])
        topi = sb("topi", [128, 2, FH, TOPK], U32)
        topf = sb("topf", [128, 2, FH, TOPK])
        cand = sb("cand", [128, FH, TOPK, TOPK])
        best = sb("best", [128, FH, TOPK])
        besti = sb("besti", [128, FH, TOPK], U32)
        sel = sb("sel", [128, 2, FH, TOPK], U32)
        self_ = sb("self_", [128, 2, FH, TOPK])
        pick = sb("pick", [128, 2, FH, TOPK])
        oneh = sb("oneh", [128, FH, TOPK, TOPK])
        iota_rep = sb("iota_rep", [128, 128, ROUND], F16)
        over = sb("over", [128, FH, TOPK])
        ex = sb("ex", [128, TILES, FH, TOPK])
        den = sb("den", [128, TILES, FH])
        pack = sb("pack", [128, TILES, 4, SLOTS], F16)
        packT = sb("packT", [128, TILES, 4, TT], F16)
        eqx = sb("eqx", [128, 2, EX, ROUND], F16)
        fin = xn
        sg = slots[:, 6 * D:6 * D + T]
        kT = slots[:, 0:DC * T].rearrange("p (a t) -> p a t", a=DC)

        ps = ctx.enter_context(nc.psum_tensor("ps", [128, 8, 512], F32))

        def flat(bank, width):
            return ps[:, bank:bank + 2, :].rearrange("p a c -> p (a c)")[:, 0:width]

        def halves(tile):
            return tile.rearrange("p (a t) -> p a t", a=2)

        h_dram = nc.dram_tensor("h_scratch", (T, D), F32, kind="Internal").ap()

        ld_con, ld_wtok, ld_pos, ld_bias = sem("ld_con"), sem("ld_wtok"), sem("ld_pos"), sem("ld_bias")
        ld_x = [sem(f"ld_x{c}") for c in range(CIN)]
        ld_qkv, ld_wo, ld_nat, ld_ue = sem("ld_qkv"), sem("ld_wo"), sem("ld_nat"), sem("ld_ue")
        ld_de = [sem("ld_de0"), sem("ld_de1")]
        ld_res, st_h = sem("ld_res"), sem("st_h")
        st_out = [sem("st_out0"), sem("st_out1")]
        var_ready, rstd_ready = sem("var_ready"), sem("rstd_ready")
        dve_chain, pool_chain = sem("dve_chain"), sem("pool_chain")
        s_const, s_zero = sem("s_const"), sem("s_zero")
        ld_gated, pe_gated, act_gated, gated_lo = sem("ld_gated"), sem("pe_gated"), sem("act_gated"), sem("gated_lo")
        pe_nat, act_nat, re_dve, re_act = sem("pe_nat"), sem("act_nat"), sem("re_dve"), sem("re_act")
        pe_patch, patch_dve, patch_act = sem("pe_patch"), sem("patch_dve"), sem("patch_act")
        pe_emb, xn_ready, pe_xn, xnT_ready = sem("pe_emb"), sem("xn_ready"), sem("pe_xn"), sem("xnT_ready")
        kexp_pool, q_ready, pe_qk, rope_done, kT_ready, kexp_dve, kexp_act = (
            sem("kexp_pool"), sem("q_ready"), sem("pe_qk"), sem("rope_done"), sem("kT_ready"), sem("kexp_dve"), sem("kexp_act"))
        pe_vT, vT_ready, pe_v, v_dve, v_act = sem("pe_vT"), sem("vT_ready"), sem("pe_v"), sem("v_dve"), sem("v_act")
        pe_sc, sc_sub, exp_done, prob_ready = sem("pe_sc"), sem("sc_sub"), sem("exp_done"), sem("prob_ready")
        pe_pT, pT_ready, pe_o, oT_ready, pe_wo = (
            sem("pe_pT"), sem("pT_ready"), sem("pe_o"), sem("oT_ready"), sem("pe_wo"))
        hn_ready, pe_hn, hnT_ready, hn_lo_ready, h_ready = (
            sem("hn_ready"), sem("pe_hn"), sem("hnT_ready"), sem("hn_lo_ready"), sem("h_ready"))
        pe_q, qT_ready, pe_sim, sim_read = sem("pe_q"), sem("qT_ready"), sem("pe_sim"), sem("sim_read")
        pe_gate, pe_gu, gate_act, gu_done = (
            sem("pe_gate"), sem("pe_gu"), sem("gate_act"), sem("gu_done"))
        split_ready = sem("split_ready")
        pe_deT, deT_ready, pe_s, sil_ready = sem("pe_deT"), sem("deT_ready"), sem("pe_s"), sem("sil_ready")
        lg_ready, lg_exp, slots_ready = sem("lg_ready"), sem("lg_exp"), sem("slots_ready")
        eqx_ready, a_pool = sem("eqx_ready"), sem("a_pool")
        pe_p, g_ready, pe_out, fin_ready = sem("pe_p"), sem("g_ready"), sem("pe_out"), sem("fin_ready")

        rounds = [(j, t0, min(ROUND, valid(j) - t0)) for j in range(TILES) for t0 in range(0, valid(j), ROUND)]
        POOL_Q = 2
        NG = len(GROUPS)

        def weigh(engine, i, q):
            j, t0, w = rounds[i]
            own = slice(SLOTS * q, SLOTS * (q + 1))
            return engine.tensor_tensor(
                A[own, i % RING, :, q, :, 0:w],
                eqx[own, i % 2, :, 0:w].unsqueeze(1).broadcast_to([SLOTS, 2, EX, w]),
                packT[own, j, 2:4, t0:t0 + w].unsqueeze(2).broadcast_to([SLOTS, 2, EX, w]), ALU.mult)
        NG_BANKS = 6

        def load_experts(queue, e2, slot):
            queue.dma_start(de[:, slot, :, :],
                            down_e[bass.ds(e2 * 256, 256), :].rearrange("(a p) n -> p a n", p=128)
                            ).then_inc(ld_de[slot], 16)

        def load_pixels(queue, c):
            queue.dma_start(x_sb[0:SIDE * B, c].rearrange("p a w -> p (a w)"),
                            x[:, c, :, :].rearrange("b (r a) w -> r b (a w)", r=SIDE)).then_inc(ld_x[c], 16)

        block = ctx.enter_context(nc.Block())

        @block.sync
        def _(sp):
            for c in range(CIN - 1):
                load_pixels(sp, c)
            sp.dma_start(posful[0:ROWS, :], pos[0:1, :, :].broadcast_to([PER, S, D])).then_inc(ld_pos, 16)
            sp.dma_start(addend[0:ROWS, :], b_tok.rearrange("(a n) -> a n", a=1).broadcast_to([ROWS, D])
                         ).then_inc(ld_bias, 16)
            sp.wait_ge(ld_bias, 16)
            sp.dma_start(addend[0:ROWS:S, :], cls_tok[0, :, :].broadcast_to([PER, D])).then_inc(ld_pos, 16)
            sp.dma_start(wqkv[:, :, :], w_qkv.rearrange("(k p) n -> p k n", p=128)).then_inc(ld_qkv, 16)
            sp.dma_start(wq_nat, w_queries.rearrange("(a p) n -> p a n", p=128)).then_inc(ld_nat, 16)
            for p in range(2):
                sp.dma_start(keys_nat[:, p], keys[:, :, p, :].rearrange("h k n -> k h n")).then_inc(ld_nat, 16)
            sp.dma_start(wo[:, :, :], w_o.rearrange("(k p) n -> p k n", p=128)).then_inc(ld_wo, 16)
            for e2 in range(2):
                load_experts(sp, e2, e2)
            sp.wait_ge(pe_v, B // 2)
            sp.dma_start(gate_nat, w_gate.rearrange("(a p) n -> p a n", p=128)).then_inc(ld_gated, 16)
            sp.dma_start(up_nat, w_up.rearrange("(a p) n -> p a n", p=128)).then_inc(ld_gated, 16)
            sp.dma_start(down_nat, w_down.rearrange("(a p) n -> p a n", p=128)).then_inc(ld_gated, 16)
            for gi, (b0, n) in enumerate(GROUPS):
                sp.wait_ge(h_ready, gi + 1)
                sp.dma_start(h_dram[b0 * S:(b0 + n) * S, :], h[0:n * S, gi, :]).then_inc(st_h, 16)
            up_v = up_e.rearrange("(e p) n -> p e n", p=128)
            w = EX // 4

            def load_up(c):
                sp.wait_ge(pe_wo, NG)
                sp.dma_start(ue[:, bass.ds(c * w, w), :], up_v[:, bass.ds(c * w, w), :]).then_inc(ld_ue, 16)

            with sp.Fori(0, 3) as c:
                for i in range(4):
                    sp.wait_ge(split_ready, c * 8 + 2 * (i + 1))
                    load_experts(sp, c * 4 + (i + 2), i % 2)
                load_up(c)
            for e2 in range(14, EX // 2):
                sp.wait_ge(split_ready, 2 * (e2 - 1))
                load_experts(sp, e2, e2 % 2)
            load_up(3)
            sp.wait_ge(st_h, 16 * NG)
            sp.wait_ge(pe_s, EX)
            for j in range(TILES):
                r = Q * valid(j)
                sp.dma_start(resid[0:r, j, :], h_dram[j * 128:j * 128 + r, :]).then_inc(ld_res, 16)
            for j in range(TILES):
                r = Q * valid(j)
                sp.wait_ge(fin_ready, j + 1)
                sp.dma_start(out[j * 128:j * 128 + r, :], fin[0:r, j % 2, :]).then_inc(st_out[j % 2], 16)
            for i in range(2):
                sp.wait_ge(st_out[i], 16 * len(range(i, TILES, 2)))

        @block.gpsimd
        def _(pool):
            nc.gpsimd.memset(patchT.rearrange("p k (b s) -> p k b s", s=S)[:, :, :, 0:1], 0.0).then_inc(s_zero, 1)
            nc.gpsimd.memset(nhalf[:, :], -0.5).then_inc(pool_chain, 1)
            nc.gpsimd.memset(qpad, 0.0).then_inc(s_zero, 1)
            nc.gpsimd.memset(keysBD[:, :, :, :], 0.0).then_inc(s_zero, 1)
            nc.gpsimd.memset(qT[:, :, (TILES - 1) * 128:TP], 0.0).then_inc(s_zero, 1)

            def rstd(i, gi):
                r = GROUPS[gi][1] * S
                pool.wait_ge(var_ready, i + 1)
                nc.gpsimd.tensor_scalar(veps[0:r, :], mv[0:r, 1:2], EPS, None, ALU.add).then_inc(pool_chain, 1)
                pool.wait_ge(pool_chain, i + 2)
                nc.gpsimd.tensor_tensor(rs[0:r, :], veps[0:r, :], nhalf[0:r, :], ALU.pow).then_inc(rstd_ready, 1)

            for gi in range(NG):
                rstd(gi, gi)
            for a in range(2):
                pool.wait_ge(kT_ready, 2 * (a + 1))
                for hh in POOL_HEADS:
                    head = con[:, C_HEAD + hh:C_HEAD + hh + 1].unsqueeze(2).broadcast_to([128, B, S])
                    nc.gpsimd.tensor_tensor(kexp[:, a, :, hh, :], kT[:, a, :].rearrange("p (b s) -> p b s", s=S),
                                            head, ALU.mult).then_inc(kexp_pool, 1)
            for i in range(EX // 2):
                if i == 2:
                    for gi in range(NG):
                        rstd(NG + gi, gi)
                if EX // 2 - 4 <= i < EX // 2 - 2:
                    pool.wait_ge(pe_sim, 2 * TILES)
                    pool.wait_ge(pe_gu, IC)
                    w = slot_a_words // 2
                    n = i - EX // 2 + 4
                    nc.gpsimd.memset(late[:, n * w:(n + 1) * w], 0.0).then_inc(s_zero, 1)
                pool.wait_ge(ld_de[i % 2], 16 * (i // 2 + 1))
                if i >= 2:
                    pool.wait_ge(pe_deT, 2 * (i - 1))
                nc.gpsimd.tensor_copy(de_hi[:, i % 2], de[:, i % 2]).then_inc(split_ready, 1)
                pool.wait_ge(split_ready, 2 * i + 1)
                nc.gpsimd.tensor_tensor(de_lo[:, i % 2], de[:, i % 2], de_hi[:, i % 2].bitcast(F32),
                                        ALU.subtract).then_inc(split_ready, 1)
            for i in range(RING, len(rounds)):
                pool.wait_ge(eqx_ready, i + 1)
                for q in range(Q - POOL_Q, Q):
                    weigh(nc.gpsimd, i, q).then_inc(a_pool, 1)

        @block.scalar
        def _(act):
            act.dma_start(con[:, :], consts[:, :]).then_inc(ld_con, 16)
            load_pixels(act, CIN - 1)
            act.dma_start(wtok[:, :, :], w_tok.rearrange("(k p) n -> p k n", p=128)).then_inc(ld_wtok, 16)
            act.wait_ge(ld_con, 16)
            nc.scalar.copy(ident_h[:, :], ident).then_inc(s_const, 1)
            nc.scalar.copy(ident_r[:, :], ident).then_inc(s_const, 1)
            nc.scalar.copy(causal_h[:, :], con[:, C_CAUSAL:C_CAUSAL + S]).then_inc(s_const, 1)
            act.wait_ge(ld_x[CIN - 1], 16)
            for w in range(SIDE):
                nc.scalar.copy(x_re[0:SIDE * B, CIN - 1, w, :].rearrange("p (r n) -> p r n", r=PATCH),
                               x_sb[0:SIDE * B, CIN - 1, :, w * PATCH:(w + 1) * PATCH]).then_inc(re_act, 1)
            act.wait_ge(s_zero, 1)
            for u in range(1, 2 * KC_TOK, 2):
                act.wait_ge(pe_patch, u + 1)
                kc, half = divmod(u, 2)
                dst = patchT[:, kc, :].rearrange("p (b s) -> p b s", s=S)[:, :, 1:]
                dst = dst.rearrange("p b (r c) -> p c r b", c=SIDE)[:, 3 * half:3 * half + 3]
                nc.scalar.copy(dst, ps[:, u % 8, 0:3 * SIDE * B].rearrange("p (c r b) -> p c r b", c=3, b=B)
                               ).then_inc(patch_act, 1)
            nc.scalar.copy(iota_rep[:, :, :], con[:, C_IOTA:C_IOTA + 128].unsqueeze(2).broadcast_to([128, 128, ROUND])
                           ).then_inc(s_const, 1)
            def xn_copy(gi):
                b0, n = GROUPS[gi]
                act.wait_ge(pe_xn, gi + 1)
                r = n * S
                nc.scalar.copy(xnT[:, :, b0 * S:b0 * S + r],
                               ps[:, 6 + gi % 2, 0:2 * r].rearrange("p (k t) -> p k t", k=2)).then_inc(xnT_ready, 1)

            for gi in range(NG - 2):
                xn_copy(gi)
            act.wait_ge(pe_nat, 1)
            nc.scalar.copy(wqT[:, :, :].rearrange("p k (a b) -> p (k a) b", a=2),
                           ps[:, 4, :].rearrange("p (a b) -> p a b", a=4)).then_inc(act_nat, 1)
            xn_copy(NG - 2)
            act.wait_ge(pe_nat, 2)
            act.wait_ge(s_zero, 3)
            for hh in range(FH):
                nc.scalar.copy(keysBD[32 * hh:32 * hh + 32, :, hh, :],
                               ps[32 * hh:32 * hh + 32, 5, 0:256].rearrange("p (a b) -> p a b", a=2)
                               ).then_inc(act_nat, 1)
            xn_copy(NG - 1)

            def gated_copy(u):
                act.wait_ge(pe_gated, u + 1)
                src = ps[:, u % 2, :].rearrange("p (a b) -> p a b", a=4)
                if u // 2 == 1:
                    dst = downT[:, 2 * (u - 2):2 * (u - 2) + 2, :].rearrange("p k (a b) -> p (k a) b", a=2)
                else:
                    dst = (gate_hi, None, up_hi)[u // 2][:, u % 2, :].rearrange("p (a b) -> p a b", a=4)
                nc.scalar.copy(dst, src).then_inc(act_gated, 1)

            def spread(a):
                act.wait_ge(kT_ready, 2 * (a + 1))
                for hh in ACT_HEADS:
                    nc.scalar.mul(kexp[:, a, :, hh, :], kT[:, a, :].rearrange("p (b s) -> p b s", s=S),
                                  con[:, C_HEAD + hh:C_HEAD + hh + 1]).then_inc(kexp_act, 1)

            for c in range(DC):
                act.wait_ge(pe_vT, c + 1)
                src = ps[:, 2 * c:2 * c + 2, 0:HALF].rearrange("p a (b s) -> p a b s", s=S)
                for i in range(2):
                    nc.scalar.copy(vT[:, c, :, i, :].rearrange("p (a b) s -> p a b s", a=2), src
                                   ).then_inc(vT_ready, 1)
                spread(c)

            def values(u):
                act.wait_ge(pe_v, u + 1)
                for e in range(2):
                    nc.scalar.mul(
                        vblk[0:2 * S, 2 * u:2 * u + 2, :].rearrange("p b (c e d) -> p (b c) e d", e=2, d=DK)[:, :, e],
                        ps[0:2 * S, 2 + u % 6, :].rearrange("p (c e d) -> p c e d", e=2, d=DK)[:, :, e],
                        con[0:2 * S, C_PAR + e * DK:C_PAR + e * DK + 1]).then_inc(v_act, 1)

            def exponentials(gi):
                r = GROUPS[gi][1] * S
                act.wait_ge(sc_sub, gi + 1)
                nc.scalar.activation(pr[0:r, gi % 2], pr[0:r, gi % 2], ACT.Exp,
                                     scale=DK ** -0.5).then_inc(exp_done, 1)

            def hn_copy(gi):
                b0, n = GROUPS[gi]
                r = n * S
                act.wait_ge(pe_hn, gi + 1)
                for dst in (hnT, hn_hi):
                    nc.scalar.copy(dst[:, :, b0 * S:b0 * S + r],
                                   ps[:, 7, 0:2 * r].rearrange("p (k t) -> p k t", k=2)).then_inc(hnT_ready, 1)

            values(1)
            values(3)
            exponentials(0)
            values(5)
            values(7)
            exponentials(1)
            for gi, (b0, n) in enumerate(GROUPS):
                r = n * S
                act.wait_ge(pe_pT, gi + 1)
                if gi >= 2:
                    act.wait_ge(pe_o, gi - 1)
                nc.scalar.copy(pT[0:2 * S, gi % 2, :, 0:r].rearrange("p (a c) r -> p a c r", a=2),
                               ps[0:2 * S, 2:4, 0:4 * r].rearrange("p a (c r) -> p a c r", c=4)
                               ).then_inc(pT_ready, 1)
                if gi >= NG - 2:
                    gated_copy(3 * (gi - NG + 2))
                act.wait_ge(pe_o, gi + 1)
                if gi >= 2:
                    act.wait_ge(pe_wo, gi - 1)
                nc.scalar.copy(oT[:, gi % 2, :, 0:r],
                               ps[:, 4, 0:256].rearrange("p (a r) -> p a r", a=2)[:, :, 0:r]).then_inc(oT_ready, 1)
                if gi >= NG - 2:
                    gated_copy(3 * (gi - NG + 2) + 1)
                if gi >= 1:
                    hn_copy(gi - 1)
                if gi >= NG - 2:
                    gated_copy(3 * (gi - NG + 2) + 2)
                if gi + 2 < NG:
                    exponentials(gi + 2)
            def deT_copy(e):
                act.wait_ge(pe_deT, e + 1)
                if e >= 4:
                    act.wait_ge(pe_s, e - 3)
                nc.scalar.copy(deT[:, e % 4], ps[:, e % 2, :].bitcast(F32R)
                               .rearrange("p (i k y) -> p i k y", i=2, k=DC)).then_inc(deT_ready, 1)

            hn_copy(NG - 1)
            act.wait_ge(s_zero, 4)
            for p in range(2):
                act.wait_ge(pe_q, p + 1)
                nc.scalar.copy(qT[:, p, 0:BANK], ps[:, 2 + 2 * p, :]).then_inc(qT_ready, 1)
                nc.scalar.copy(qT[:, p, BANK:TP].rearrange("p (q t) -> p q t", q=Q)[:, :, 0:valid(TILES - 1)],
                               ps[:, 3 + 2 * p, 0:T - BANK].rearrange("p (q t) -> p q t", q=Q)).then_inc(qT_ready, 1)

            e = 0
            deT_copy(0)
            deT_copy(1)
            act.wait_ge(st_h, 16 * NG)
            for j, seg in enumerate(SEGS):
                for i in range(seg):
                    if j == TILES - 1 and i == 5:
                        act.wait_ge(lg_ready, TILES)
                        nc.scalar.activation(ex[:, :, :, :], ex[:, :, :, :], ACT.Exp).then_inc(lg_exp, 1)
                    if e + 2 < EX:
                        deT_copy(e + 2)
                    act.wait_ge(pe_s, e + 1)
                    nc.scalar.activation(halves(sil[:, e, :]), ps[:, 2 + 2 * (e % 2):4 + 2 * (e % 2), 0:HALF], ACT.Silu).then_inc(sil_ready, 1)
                    e += 1
                if j < IC:
                    act.wait_ge(pe_gate, j + 1)
                    if j >= 1:
                        act.wait_ge(gu_done, j)
                    nc.scalar.activation(halves(sg), ps[:, 2:4, 0:HALF], ACT.Silu).then_inc(gate_act, 1)

        @block.vector
        def _(dve):
            counts, newest = {}, []

            def chain(ins, then=dve_chain):
                counts[then] = counts.get(then, 0) + 1
                ins.then_inc(then, 1)
                newest[:] = [(then, counts[then])]

            def behind():
                dve.wait_ge(*newest[0])

            norms = [0]

            def norm(rows, src, dst, then):
                norms[0] += 1
                behind()
                chain(nc.vector.bn_stats(stats[0:rows, :], src))
                behind()
                chain(nc.vector.bn_aggr(mv[0:rows, :], stats[0:rows, :]), var_ready)
                dve.wait_ge(rstd_ready, norms[0])
                behind()
                chain(nc.vector.tensor_scalar(dst, src, mv[0:rows, 0:1], rs[0:rows, :],
                                              ALU.subtract, ALU.mult), then)

            for c in range(CIN - 1):
                dve.wait_ge(ld_x[c], 16)
                for w in range(SIDE):
                    chain(nc.vector.tensor_copy(x_re[0:SIDE * B, c, w, :].rearrange("p (r n) -> p r n", r=PATCH),
                                                x_sb[0:SIDE * B, c, :, w * PATCH:(w + 1) * PATCH]), re_dve)
            dve.wait_ge(s_zero, 1)
            for u in range(0, 2 * KC_TOK, 2):
                dve.wait_ge(pe_patch, u + 1)
                kc = u // 2
                dst = patchT[:, kc, :].rearrange("p (b s) -> p b s", s=S)[:, :, 1:]
                dst = dst.rearrange("p b (r c) -> p c r b", c=SIDE)[:, 0:3]
                chain(nc.vector.tensor_copy(dst, ps[:, u % 8, 0:3 * SIDE * B]
                                            .rearrange("p (c r b) -> p c r b", c=3, b=B)), patch_dve)
            dve.wait_ge(ld_pos, 16 * 2)
            chain(nc.vector.tensor_tensor(posful[0:ROWS, :], posful[0:ROWS, :], addend[0:ROWS, :], ALU.add))
            for gi, (b0, n) in enumerate(GROUPS):
                r = n * S
                dve.wait_ge(pe_emb, gi + 1)
                behind()
                chain(nc.vector.tensor_tensor(h[0:r, gi, :], ps[0:r, (4 + gi) % NG_BANKS, 0:D], posful[0:r, :], ALU.add))
                if gi >= 2:
                    dve.wait_ge(pe_xn, gi - 1)
                norm(r, h[0:r, gi, :], xn[0:r, gi % 2, :], xn_ready)
            cosb = con[:, C_COS:C_COS + S].unsqueeze(1).unsqueeze(1).broadcast_to([128, 2, B // 2, S])
            sinb = con[:, C_SIN:C_SIN + S].unsqueeze(1).unsqueeze(1).broadcast_to([128, 2, B // 2, S])

            def rotate(t):
                dve.wait_ge(pe_qk, t + 1)
                for i, (odd, table) in enumerate(((0, cosb), (1, sinb), (0, sinb), (1, cosb))):
                    src = ps[:, 4 * t + odd:4 * t + 4:2, 0:HALF].rearrange("p a (b s) -> p a b s", s=S)
                    behind()
                    chain(nc.vector.tensor_tensor(rot[:, i, :].rearrange("p (a b s) -> p a b s", a=2, s=S),
                                                  src, table, ALU.mult), rope_done if i == 3 else dve_chain)
                behind()

            def pieces(a):
                heads = slice(64 * a, 64 * a + 64)
                return ((heads, slice(0, 64), 0, ALU.subtract), (heads, slice(64, 128), 2, ALU.add))

            rotate(0)
            for a in range(2):
                for src, dst, i, op in pieces(a):
                    chain(nc.vector.tensor_tensor(kT[dst, a, :], rot[src, i, :], rot[src, i + 1, :], op), kT_ready)
            rotate(1)
            dve.wait_ge(s_zero, 2)
            for a in range(2):
                window = qpad[:, a, :].rearrange("p (i x) -> p i x", i=PER)[:, :, 0:FULL * ROWS]
                window = window.rearrange("p i (g r) -> p i g r", g=FULL)[:, :, :, 0:S]
                for src, dst, i, op in pieces(a):
                    v = [rot[src, i + n, 0:FULL * ROWS].rearrange("p (g i s) -> p i g s", i=PER, s=S)
                         for n in range(2)]
                    chain(nc.vector.tensor_tensor(window[dst], v[0], v[1], op), q_ready)
                    chain(nc.vector.tensor_tensor(q_left[dst, a, :], rot[src, i, FULL * ROWS:T],
                                                  rot[src, i + 1, FULL * ROWS:T], op), q_ready)
            behind()
            for a in range(2):
                for hh in range(HP):
                    if hh in ACT_HEADS + POOL_HEADS:
                        continue
                    chain(nc.vector.tensor_scalar(kexp[:, a, :, hh, :], kT[:, a, :].rearrange("p (b s) -> p b s", s=S),
                                                  con[:, C_HEAD + hh:C_HEAD + hh + 1], None, ALU.mult), kexp_dve)
            par = con[0:2 * S, C_PAR:C_PAR + 2 * DK].unsqueeze(1).broadcast_to([2 * S, 2 * PAIRS, 2 * DK])

            def values(u):
                dve.wait_ge(pe_v, u + 1)
                chain(nc.vector.tensor_tensor(
                    vblk[0:2 * S, 2 * u:2 * u + 2, :].rearrange("p b (c d) -> p (b c) d", d=2 * DK),
                    ps[0:2 * S, 2 + u % 6, :].rearrange("p (c d) -> p c d", d=2 * DK), par, ALU.mult), v_dve)

            def softmax_front(gi):
                r = GROUPS[gi][1] * S
                dve.wait_ge(pe_sc, gi + 1)
                if gi >= 2:
                    dve.wait_ge(pe_pT, gi - 1)
                sc = ps[0:r, 0:2, 0:HALF].rearrange("p a (h s) -> p a h s", s=S)
                behind()
                chain(nc.vector.tensor_reduce(red[0:r, 0, :].rearrange("p (a h) -> p a h", a=2), sc, AX.X, ALU.max))
                behind()
                chain(nc.vector.tensor_tensor(pr[0:r, gi % 2].rearrange("p (a h) s -> p a h s", a=2), sc,
                                              red[0:r, 0, :].rearrange("p (a h) -> p a h", a=2).unsqueeze(3)
                                              .broadcast_to([r, 2, HP, S]), ALU.subtract), sc_sub)

            def softmax_back(gi):
                r = GROUPS[gi][1] * S
                dve.wait_ge(exp_done, gi + 1)
                behind()
                chain(nc.vector.tensor_reduce(red[0:r, 1, :], pr[0:r, gi % 2], AX.X, ALU.add))
                behind()
                chain(nc.vector.reciprocal(red[0:r, 2, :], red[0:r, 1, :]))
                behind()
                chain(nc.vector.tensor_tensor(pr[0:r, gi % 2], pr[0:r, gi % 2],
                                              red[0:r, 2, :].unsqueeze(2).broadcast_to([r, H, S]), ALU.mult),
                      prob_ready)

            def hidden(gi):
                r = GROUPS[gi][1] * S
                dve.wait_ge(pe_wo, gi + 1)
                behind()
                chain(nc.vector.tensor_tensor(h[0:r, gi, :], ps[0:r, 5 + gi % 2, 0:D], h[0:r, gi, :], ALU.add), h_ready)
                if gi >= 2:
                    dve.wait_ge(pe_hn, gi - 1)
                norm(r, h[0:r, gi, :], xn[0:r, gi % 2, :], hn_ready)

            def gated_rest(u):
                dve.wait_ge(act_gated, u + 1)
                hi, lo = ((gate_hi, gate_lo), None, (up_hi, up_lo))[u // 2]
                behind()
                chain(nc.vector.tensor_tensor(lo[:, u % 2, :], ps[:, u % 2, :], hi[:, u % 2, :].bitcast(F32),
                                              ALU.subtract), gated_lo)

            values(0)
            softmax_front(0)
            values(2)
            values(4)
            softmax_back(0)
            values(6)
            softmax_front(1)
            for gi in range(1, NG):
                softmax_back(gi)
                if gi + 1 < NG:
                    softmax_front(gi + 1)
                else:
                    gated_rest(0)
                    gated_rest(1)
                hidden(gi - 1)
            hidden(NG - 1)
            gated_rest(4)
            gated_rest(5)
            for groups in (range(NG - 1), range(NG - 1, NG)):
                dve.wait_ge(hnT_ready, 2 * (groups.stop))
                cols = slice(groups.start * ROWS, min(T, groups.stop * ROWS))
                chain(nc.vector.tensor_tensor(hn_lo[:, :, cols], hnT[:, :, cols], hn_hi[:, :, cols].bitcast(F32),
                                              ALU.subtract), hn_lo_ready)

            iota8 = con[:, C_IOTA:C_IOTA + TOPK]

            def build_slots(i):
                j, t0, w = rounds[i]
                if i == 0:
                    dve.wait_ge(s_zero, 6)
                if i >= RING:
                    dve.wait_ge(pe_p, i - RING + 1)
                s_i = i % RING
                behind()
                chain(nc.vector.tensor_tensor(R[:, s_i, :, 0:w], iota_rep[:, :, 0:w],
                                              packT[:, j, 1, t0:t0 + w].unsqueeze(1).broadcast_to([128, 128, w]),
                                              ALU.is_equal))
                if i >= RING + 2:
                    dve.wait_ge(a_pool, POOL_Q * (i - RING - 1))
                chain(nc.vector.tensor_tensor(eqx[:, i % 2, :, 0:w], iota_rep[:, 0:EX, 0:w],
                                              packT[:, j, 0, t0:t0 + w].unsqueeze(1).broadcast_to([128, EX, w]),
                                              ALU.is_equal), eqx_ready)
                behind()
                for q in range(Q if i < RING else Q - POOL_Q):
                    chain(weigh(nc.vector, i, q), slots_ready)

            for j in range(TILES):
                for p in range(2):
                    dve.wait_ge(pe_sim, 2 * j + p + 1)
                    simv = ps[:, 6 + p, :].rearrange("p (h k) -> p h k", h=FH)
                    behind()
                    for hh in range(FH):
                        chain(nc.vector.max(top[:, p, hh, :], simv[:, hh, :]))
                    behind()
                    for hh in range(FH):
                        chain(nc.vector.max_index(topi[:, p, hh, :], top[:, p, hh, :], simv[:, hh, :]),
                              sim_read if hh == FH - 1 else dve_chain)
                behind()
                chain(nc.vector.tensor_copy(topf[:, :, :, :], topi[:, :, :, :]))
                chain(nc.vector.tensor_tensor(cand[:, :, :, :],
                                              top[:, 0].unsqueeze(3).broadcast_to([128, FH, TOPK, TOPK]),
                                              top[:, 1].unsqueeze(2).broadcast_to([128, FH, TOPK, TOPK]), ALU.add))
                behind()
                cf = cand[:, :, :, :].rearrange("p h i j -> p h (i j)")
                for hh in range(FH):
                    chain(nc.vector.max(best[:, hh, :], cf[:, hh, :]))
                behind()
                for hh in range(FH):
                    chain(nc.vector.max_index(besti[:, hh, :], best[:, hh, :], cf[:, hh, :]))
                chain(nc.vector.tensor_tensor(ex[:, j], best[:, :, :],
                                              best[:, :, 0:1].broadcast_to([128, FH, TOPK]), ALU.subtract), lg_ready)
                behind()
                chain(nc.vector.tensor_scalar(sel[:, 0], besti[:, :, :], 3, None, ALU.logical_shift_right))
                chain(nc.vector.tensor_scalar(sel[:, 1], besti[:, :, :], TOPK - 1, None, ALU.bitwise_and))
                behind()
                chain(nc.vector.tensor_copy(self_[:, :, :, :], sel[:, :, :, :]))
                for p in range(2):
                    behind()
                    chain(nc.vector.tensor_tensor(oneh[:, :, :, :],
                                                  self_[:, p].unsqueeze(3).broadcast_to([128, FH, TOPK, TOPK]),
                                                  iota8.unsqueeze(1).unsqueeze(1).broadcast_to([128, FH, TOPK, TOPK]),
                                                  ALU.is_equal))
                    behind()
                    chain(nc.vector.tensor_tensor(oneh[:, :, :, :], oneh[:, :, :, :],
                                                  topf[:, p].unsqueeze(2).broadcast_to([128, FH, TOPK, TOPK]),
                                                  ALU.mult))
                    behind()
                    chain(nc.vector.tensor_reduce(pick[:, p], oneh[:, :, :, :], AX.X, ALU.add))
                behind()
                chain(nc.vector.tensor_scalar(over[:, :, :], pick[:, 0], float(EX), float(NK - 1), ALU.is_ge, ALU.mult))
                chain(nc.vector.tensor_scalar(pack[:, j, 0, :].rearrange("p (h k) -> p h k", h=FH), pick[:, 0],
                                              float(EX - 1), None, ALU.min))
                behind()
                chain(nc.vector.tensor_tensor(pack[:, j, 1, :].rearrange("p (h k) -> p h k", h=FH), pick[:, 1],
                                              over[:, :, :], ALU.max))
                if j < IC:
                    dve.wait_ge(gate_act, j + 1)
                    dve.wait_ge(pe_gu, j + 1)
                    chain(nc.vector.scalar_tensor_tensor(halves(actT[:, j, :]), halves(sg), WSCALE,
                                                         ps[:, 4:6, 0:HALF], ALU.mult, ALU.mult), gu_done)
            dve.wait_ge(lg_exp, 1)
            exf = ex[:, :, :, :].rearrange("p j h k -> p (j h) k")
            denf = den[:, :, :].rearrange("p j h -> p (j h)")
            chain(nc.vector.tensor_reduce(denf, exf, AX.X, ALU.add))
            behind()
            chain(nc.vector.reciprocal(denf, denf))
            behind()
            chain(nc.vector.scalar_tensor_tensor(exf, exf, WSCALE,
                                                 denf.unsqueeze(2).broadcast_to([128, TILES * FH, TOPK]),
                                                 ALU.mult, ALU.mult))
            behind()
            wj = ex[:, :, :, :].rearrange("p j h k -> p j (h k)")
            chain(nc.vector.tensor_copy(pack[:, :, 2, :], wj))
            behind()
            chain(nc.vector.tensor_tensor(pack[:, :, 3, :], wj, pack[:, :, 2, :], ALU.subtract))
            behind()
            chain(nc.vector.transpose(packT[:, :, :, :].rearrange("p j a t -> p (j a t)"),
                                      pack[:, :, :, :].rearrange("p j a s -> p (j a s)")))
            for i in range(RING):
                build_slots(i)
            dve.wait_ge(sil_ready, EX)
            n_p = 0

            def finish(j):
                v = valid(j)
                dve.wait_ge(pe_out, j + 1)
                if j == 0:
                    dve.wait_ge(ld_res, 16 * TILES)
                if j >= 2:
                    dve.wait_ge(st_out[j % 2], 16 * (j // 2))
                chain(nc.vector.scalar_tensor_tensor(fin[0:Q * v, j % 2, :], ps[0:Q * v, 4 + j % 2, 0:D],
                                                     1.0 / WSCALE, resid[0:Q * v, j, :], ALU.mult, ALU.add),
                      fin_ready)

            for i, (j, t0, w) in enumerate(rounds):
                dve.wait_ge(pe_p, i + 1)
                pv = flat(2 * (i % 2), Q * EX * w).rearrange("p (t q e) -> p q e t", e=EX, q=Q)
                dst = sil[:, :, j * 128:j * 128 + Q * valid(j)].rearrange("p e (q t) -> p q e t", q=Q)
                dst = dst[:, :, :, t0:t0 + w]
                behind()
                chain(nc.vector.tensor_tensor(dst, pv, dst, ALU.mult), g_ready)
                if i == RING - 1:
                    for ahead in range(RING, 2 * RING):
                        build_slots(ahead)
                elif RING <= i < len(rounds) - RING:
                    build_slots(i + RING)
                if t0 + w == valid(j) and j >= 1:
                    finish(j - 1)
            finish(TILES - 1)

        @block.tensor
        def _(pe):
            mm, tr = nc.tensor.matmul, nc.tensor.transpose
            pe.wait_ge(ld_con, 16)
            for u in range(2 * KC_TOK):
                kc, half = divmod(u, 2)
                c, px = kc // 2, slice(128 * (kc % 2), 128 * (kc % 2) + 128)
                if u >= 8:
                    pe.wait_ge((patch_dve, patch_act)[u % 2], u // 2 - 3)
                for wp in range(3):
                    if kc % 2 == 0:
                        if c < CIN - 1:
                            pe.wait_ge(re_dve, SIDE * c + 3 * half + wp + 1)
                        else:
                            pe.wait_ge(re_act, 3 * half + wp + 1)
                    last = tr(ps[:, u % 8, wp * SIDE * B:(wp + 1) * SIDE * B],
                              x_re[0:SIDE * B, c, 3 * half + wp, px], ident[0:SIDE * B, 0:SIDE * B])
                last.then_inc(pe_patch, 1)
            pe.wait_ge(patch_dve, KC_TOK)
            pe.wait_ge(patch_act, KC_TOK)
            pe.wait_ge(ld_wtok, 16)

            def rows_T(gi, ready, bank, done):
                r = GROUPS[gi][1] * S
                pe.wait_ge(ready, gi + 1)
                for k in range(DC):
                    last = tr(ps[:, bank, k * r:(k + 1) * r], xn[0:r, gi % 2, k * 128:(k + 1) * 128],
                              ident[0:r, 0:r])
                last.then_inc(done, 1)

            for gi, (b0, n) in enumerate(GROUPS):
                r = n * S
                for k in range(KC_TOK):
                    last = mm(ps[0:r, (4 + gi) % NG_BANKS, 0:D], patchT[:, k, b0 * S:b0 * S + r], wtok[:, k, :],
                              start=(k == 0), stop=(k == KC_TOK - 1))
                last.then_inc(pe_emb, 1)
                if gi >= 2:
                    if gi >= 4:
                        pe.wait_ge(xnT_ready, gi - 3)
                    rows_T(gi - 2, xn_ready, 6 + gi % 2, pe_xn)
            pe.wait_ge(ld_nat, 16 * 3)
            for i, (a, k) in enumerate(((0, 0), (1, 0), (0, 1), (1, 1))):
                last = tr(ps[:, 4, i * 128:(i + 1) * 128], wq_nat[:, a, k * 128:(k + 1) * 128], ident)
            last.then_inc(pe_nat, 1)
            for p in range(2):
                last = tr(ps[:, 5, p * 128:(p + 1) * 128], keys_nat[:, p].rearrange("p h n -> p (h n)"), ident)
            last.then_inc(pe_nat, 1)
            pe.wait_ge(xnT_ready, NG - 3)
            rows_T(NG - 2, xn_ready, 6 + NG % 2, pe_xn)

            def rope_input(t, a, odd):
                base = (D, 0)[t]
                for k in range(DC):
                    last = mm(ps[:, 4 * t + 2 * a + odd, 0:HALF], wqkv[:, k, base + odd:base + D:2],
                              xnT[:, k, a * HALF:(a + 1) * HALF], start=(k == 0), stop=(k == DC - 1))
                return last

            pe.wait_ge(ld_qkv, 16)
            for odd in range(2):
                rope_input(0, 0, odd)
            pe.wait_ge(xnT_ready, NG - 2)
            rows_T(NG - 1, xn_ready, 6 + (NG - 1) % 2, pe_xn)
            pe.wait_ge(act_nat, 1)
            rope_input(1, 0, 0)
            pe.wait_ge(xnT_ready, NG)
            rope_input(0, 1, 0)
            rope_input(0, 1, 1).then_inc(pe_qk, 1)
            pe.wait_ge(act_nat, 1 + FH)
            rope_input(1, 0, 1)
            rope_input(1, 1, 0)
            rope_input(1, 1, 1).then_inc(pe_qk, 1)
            pe.wait_ge(rope_done, 1)
            for c in range(DC):
                for a in range(2):
                    for k in range(DC):
                        last = mm(ps[:, 2 * c + a, 0:HALF], wqkv[:, k, 2 * D + c * 128:2 * D + (c + 1) * 128],
                                  xnT[:, k, a * HALF:(a + 1) * HALF], start=(k == 0), stop=(k == DC - 1))
                last.then_inc(pe_vT, 1)

            def values(u):
                for i in range(2):
                    b = 2 * u + i
                    for c in range(DC):
                        last = tr(ps[0:2 * S, 2 + u % 6, i * D + c * 128:i * D + (c + 1) * 128],
                                  vT[:, c, b, :, :].rearrange("p two s -> p (two s)"), ident)
                last.then_inc(pe_v, 1)

            def scores(gi, a):
                b0, n = GROUPS[gi]
                r = n * S
                if gi >= 1 and a == 0:
                    pe.wait_ge(sc_sub, gi)
                bank = a
                mm(ps[0:r, bank, 0:HALF], ident_h[0:r, 0:r],
                   causal_h[0:r, :].unsqueeze(1).broadcast_to([r, HP, S]), start=True, stop=False)
                for i in range(n):
                    w0 = (i * FULL + gi) * ROWS
                    last = mm(ps[0:r, bank, 0:HALF], qpad[:, a, w0:w0 + r] if gi < FULL else q_left[:, a, :],
                              kexp[:, a, b0 + i].rearrange("p h s -> p (h s)"), start=False, stop=(i == n - 1))
                if a == 1:
                    last.then_inc(pe_sc, 1)

            def probs_T(gi):
                r = GROUPS[gi][1] * S
                pe.wait_ge(prob_ready, gi + 1)
                if gi >= 1:
                    pe.wait_ge(pT_ready, gi)
                for c in range(PAIRS):
                    last = tr(ps[0:2 * S, 2 + c // 4, (c % 4) * r:(c % 4 + 1) * r],
                              pr[0:r, gi % 2, 2 * c:2 * c + 2, :].rearrange("p h s -> p (h s)"), ident[0:r, 0:r])
                last.then_inc(pe_pT, 1)

            def attend(gi):
                b0, n = GROUPS[gi]
                pe.wait_ge(pT_ready, gi + 1)
                if gi >= 1:
                    pe.wait_ge(oT_ready, gi)
                for i in range(n):
                    for c in range(PAIRS):
                        p0 = 32 * (c % 4)
                        col = 128 * (c // 4) + i * S
                        last = mm(ps[p0:p0 + 32, 4, col:col + S],
                                  vblk[0:2 * S, b0 + i, 32 * c:32 * c + 32],
                                  pT[0:2 * S, gi % 2, c, i * S:(i + 1) * S], start=True, stop=True,
                                  tile_position=(0, p0))
                last.then_inc(pe_o, 1)

            def project(gi):
                r = GROUPS[gi][1] * S
                pe.wait_ge(oT_ready, gi + 1)
                if gi >= 2:
                    pe.wait_ge(h_ready, gi - 1)
                for k in range(DC):
                    last = mm(ps[0:r, 5 + gi % 2, 0:D], oT[:, gi % 2, k, 0:r], wo[:, k, :], start=(k == 0),
                              stop=(k == DC - 1))
                last.then_inc(pe_wo, 1)

            pe.wait_ge(vT_ready, 4)
            pe.wait_ge(rope_done, 2)
            for u in range(6):
                values(u)
            pe.wait_ge(q_ready, 8)
            pe.wait_ge(kexp_dve, 2 * (HP - len(ACT_HEADS) - len(POOL_HEADS)))
            pe.wait_ge(kexp_pool, 2 * len(POOL_HEADS))
            pe.wait_ge(kexp_act, 2 * len(ACT_HEADS))
            pe.wait_ge(s_const, 4)
            scores(0, 0)
            scores(0, 1)
            pe.wait_ge(v_dve, 1)
            values(6)
            pe.wait_ge(v_act, 2)
            values(7)
            scores(1, 0)
            scores(1, 1)
            pe.wait_ge(v_dve, B // 4)
            pe.wait_ge(v_act, B // 2)
            pe.wait_ge(ld_wo, 16)

            def gated_T(u):
                if u == 0:
                    pe.wait_ge(ld_gated, 16 * 3)
                    pe.wait_ge(sc_sub, NG)
                if u >= 2:
                    pe.wait_ge(act_gated, u - 1)
                if u in (2, 3):
                    pe.wait_ge(gated_lo, u - 1)
                k = u % 2
                if u // 2 == 1:
                    blocks = [down_nat[:, a, kk * 128:(kk + 1) * 128] for kk in (2 * k, 2 * k + 1) for a in range(2)]
                else:
                    blocks = [(gate_nat, None, up_nat)[u // 2][:, a, k * 128:(k + 1) * 128] for a in range(4)]
                for i, src in enumerate(blocks):
                    last = tr(ps[:, u % 2, i * 128:(i + 1) * 128], src, ident)
                last.then_inc(pe_gated, 1)

            for gi in range(NG):
                spare = 3 * (gi - NG + 2)
                probs_T(gi)
                if gi + 2 < NG:
                    scores(gi + 2, 0)
                else:
                    gated_T(spare)
                attend(gi)
                if gi + 2 < NG:
                    scores(gi + 2, 1)
                else:
                    gated_T(spare + 1)
                project(gi)
                if gi >= 1:
                    if gi >= 2:
                        pe.wait_ge(hnT_ready, 2 * (gi - 1))
                    rows_T(gi - 1, hn_ready, 7, pe_hn)
                if gi + 2 >= NG:
                    gated_T(spare + 2)
            def de_T(e):
                i = (e // 2) % 2
                if e % 2 == 0:
                    pe.wait_ge(split_ready, 2 * (e // 2 + 1))
                if e >= 2:
                    pe.wait_ge(deT_ready, e - 1)
                for n, src in enumerate((de_hi, de_lo)):
                    for k in range(DC):
                        last = tr(ps[:, e % 2, (2 * n + k) * 128:(2 * n + k + 1) * 128].bitcast(F32R),
                                  src[:, i, e % 2, k * 128:(k + 1) * 128], ident_r[:, :])
                last.then_inc(pe_deT, 1)

            pe.wait_ge(hnT_ready, 2 * (NG - 1))
            rows_T(NG - 1, hn_ready, 7, pe_hn)
            pe.wait_ge(hnT_ready, 2 * NG)
            for p in range(2):
                for a in range(2):
                    for k in range(DC):
                        cols = (slice(0, BANK), slice(BANK, T))[a]
                        last = mm(ps[:, 2 + 2 * p + a, 0:cols.stop - cols.start], wqT[:, k, p * 128:(p + 1) * 128],
                                  hnT[:, k, cols],
                                  start=(k == 0), stop=(k == DC - 1))
                last.then_inc(pe_q, 1)

            def sims(j, p):
                if j >= 1:
                    pe.wait_ge(sim_read, 2 * (j - 1) + p + 1)
                mm(ps[:, 6 + p, :], qT[:, p, j * 128:(j + 1) * 128],
                   keysBD[:, p, :, :].rearrange("p h k -> p (h k)"), start=True, stop=True).then_inc(pe_sim, 1)

            pe.wait_ge(gated_lo, 3)
            de_T(0)
            pe.wait_ge(gated_lo, 4)
            de_T(1)
            pe.wait_ge(qT_ready, 2)

            def gated(bank, w, c, done):
                hi, lo = w
                for a in range(2):
                    parts = [(wt, src, k) for k in range(DC) for wt, src in ((hi, hn_hi), (hi, hn_lo), (lo, hn_hi))]
                    for n, (wt, src, k) in enumerate(parts):
                        last = mm(ps[:, bank + a, 0:HALF], wt[:, k, c * 128:(c + 1) * 128],
                                  src[:, k, a * HALF:(a + 1) * HALF], start=(n == 0), stop=(n == len(parts) - 1))
                last.then_inc(done, 1)

            pe.wait_ge(hn_lo_ready, 2)
            e = 0
            for j, seg in enumerate(SEGS):
                for i in range(seg):
                    if e + 2 < EX:
                        de_T(e + 2)
                    if j >= 1 and i < 2:
                        pe.wait_ge((gate_act, gu_done)[i], j)
                    pe.wait_ge(deT_ready, e + 1)
                    if e >= 2:
                        pe.wait_ge(sil_ready, e - 1)
                    if e == 1:
                        pe.wait_ge(qT_ready, 4)
                    for a in range(2):
                        parts = [(i, src, k) for k in range(DC) for i, src in ((0, hn_hi), (0, hn_lo), (1, hn_hi))]
                        for n, (i, src, k) in enumerate(parts):
                            last = mm(ps[:, 2 + 2 * (e % 2) + a, 0:HALF], deT[:, e % 4, i, k, :],
                                      src[:, k, a * HALF:(a + 1) * HALF], start=(n == 0), stop=(n == len(parts) - 1))
                    last.then_inc(pe_s, 1)
                    if e == 1:
                        sims(0, 0)
                        sims(0, 1)
                    e += 1
                if j < IC:
                    pe.wait_ge(sil_ready, e - 1)
                    gated(2, (gate_hi, gate_lo), j, pe_gate)
                    pe.wait_ge(sil_ready, e)
                    gated(4, (up_hi, up_lo), j, pe_gu)
                if j + 1 < TILES:
                    sims(j + 1, 0)
                    sims(j + 1, 1)
            n_p = 0

            def experts(j, lo, hi, n_g):
                v = valid(j)
                acc = ps[0:Q * v, 4 + j % 2, 0:D]
                if lo == 0:
                    if j == 0:
                        pe.wait_ge(sil_ready, EX)
                        pe.wait_ge(ld_ue, 16 * 4)
                    if j >= 2:
                        pe.wait_ge(fin_ready, j - 1)
                    for c in range(IC):
                        mm(acc, actT[:, c, j * 128:j * 128 + Q * v], downT[:, c, :], start=(c == 0), stop=False)
                    pe.wait_ge(g_ready, n_g)
                for e in range(lo, hi):
                    last = mm(acc, sil[:, e, j * 128:j * 128 + Q * v], ue[:, e, :], start=False, stop=(e == EX - 1))
                if hi == EX:
                    last.then_inc(pe_out, 1)

            for j in range(TILES):
                n_g, done = n_p, 0
                n_r = -(-valid(j) // ROUND)
                for i in range(n_r):
                    if j >= 1:
                        hi = EX * (i + 1) // n_r
                        experts(j - 1, done, hi, n_g)
                        done = hi
                    w = min(ROUND, valid(j) - i * ROUND)
                    pe.wait_ge(slots_ready, Q * (n_p + 1) if n_p < RING
                               else Q * RING + (Q - POOL_Q) * (n_p - RING + 1))
                    if n_p >= RING:
                        pe.wait_ge(a_pool, POOL_Q * (n_p - RING + 1))
                    if n_p == 1:
                        pe.wait_ge(sil_ready, EX - 1)
                    if n_p >= 2:
                        pe.wait_ge(g_ready, n_p - 1)
                    for t in range(w):
                        dense = flat(2 * (n_p % 2), 2 * BANK)[:, Q * EX * t:Q * EX * (t + 1)]
                        for a in range(2):
                            last = mm(dense, R[:, n_p % RING, :, t],
                                      A[:, n_p % RING, a, :, :, t].rearrange("p q x -> p (q x)"),
                                      start=(a == 0), stop=(a == 1))
                    last.then_inc(pe_p, 1)
                    n_p += 1
            experts(TILES - 1, 0, EX, n_p)


def constants():
    import numpy as np
    c = np.zeros((128, C_ALL), np.float32)
    c[:, C_ID:C_ID + 128] = np.eye(128)
    half = DK // 2
    freq = (1.0 / np.float32(10000.0) ** (np.arange(half, dtype=np.float32) / half)).astype(np.float32)
    ang = (np.arange(S, dtype=np.float32)[None, :] * freq[:, None]).astype(np.float32)
    pair = np.arange(128) % half
    c[:, C_COS:C_COS + S] = np.cos(ang)[pair]
    c[:, C_SIN:C_SIN + S] = np.sin(ang)[pair]
    row = np.arange(128) % S
    c[:, C_CAUSAL:C_CAUSAL + S] = np.where(np.arange(S)[None, :] <= row[:, None], 0.0, NEG)
    c[:, C_HEAD:C_HEAD + HP] = np.arange(HP)[None, :] == (np.arange(128) % 64 // half)[:, None]
    c[:, C_PAR:C_PAR + 2 * DK] = (np.arange(2 * DK) // DK)[None, :] == (np.arange(128) // S)[:, None]
    c[:, C_IOTA:C_IOTA + 128] = np.arange(128)[None, :]
    return c


_INS = ["x", "L0_tok_W", "L0_tok_b", "L0_tok_class_token", "L0_tok_pos_emb", "L0_attn_w_qkv", "L0_attn_w_o",
        "L0_ffn_w_queries", "L0_ffn_keys", "L0_ffn_down_embed", "L0_ffn_up_embed", "L0_ffn_w_gate",
        "L0_ffn_w_up", "L0_ffn_w_down"]


def kernel(**inputs):
    import numpy as _np
    import concourse.bacc as _bacc
    from concourse.bass_utils import run_bass_kernel_spmd as _run

    nc = _bacc.Bacc("TRN2", target_bir_lowering=False, num_devices=1)
    arrays, args = {}, []
    for name in _INS:
        a = _np.ascontiguousarray(inputs[name])
        arrays[f"in_{name}"] = a
        args.append(nc.dram_tensor(f"in_{name}", a.shape, mybir.dt.from_np(a.dtype), kind="ExternalInput").ap())
    c = constants()
    arrays["in_consts"] = c
    args.append(nc.dram_tensor("in_consts", c.shape, F32, kind="ExternalInput").ap())
    out = nc.dram_tensor("out_0", (T, D), F32, kind="ExternalOutput").ap()
    vit_tower(nc, *args, out)
    r = _run(nc, [arrays], core_ids=[0])
    return r.results[0]["out_0"].reshape(B, S, D)
```
